# Optimizing a Trainium2 kernel written in Bass

```python
import numpy as np
import jax
import jax.numpy as jnp

def _softmax(x, axis=-1):
    return jax.nn.softmax(x, axis=axis)

def _gelu(x):
    return jax.nn.gelu(x, approximate=True)

def _silu(x):
    return jax.nn.silu(x)

def _sigmoid(x):
    return jax.nn.sigmoid(x)

def _layernorm(x, axis=-1, eps=1e-05):
    m = jnp.mean(x, axis=axis, keepdims=True)
    v = jnp.var(x, axis=axis, keepdims=True)
    return (x - m) / jnp.sqrt(v + eps)

def _scatter_add(tgt, idx, src, axis=0):
    return tgt.at[idx].add(src)

def _segment_sum(src, seg, n):
    return jax.ops.segment_sum(src, seg, n)
kernel_name = 'mk_gnn_preln_d2_gnn_r8_a99b2c'

def setup_inputs(seed: int=0):
    np.random.seed(seed)
    _w = jnp.asarray

    def _rec_inputs():
        import jax
        import jax.numpy as jnp
        _gk = jax.random.key(seed)
        x = -0.0003713 + 1 * jax.random.normal(jax.random.fold_in(_gk, 1), (12500, 128), jnp.float32)
        src = jax.random.randint(jax.random.fold_in(_gk, 2), (400000,), 0, 12500, jnp.int32)
        dst = jnp.minimum((12500 * jax.random.uniform(jax.random.fold_in(_gk, 3), (400000,)) ** 2.0).astype(jnp.int32), 99999)
        _o = jnp.argsort(dst, stable=True)
        src = src[_o]
        dst = dst[_o]
        edge_attr_16 = 0.000254407 + 0.99978 * jax.random.normal(jax.random.fold_in(_gk, 12), (400000, 16), jnp.float32)
        edge_attr_64 = -0.000128692 + 0.999872 * jax.random.normal(jax.random.fold_in(_gk, 13), (400000, 64), jnp.float32)
        return (x, src, dst, edge_attr_16, edge_attr_64)
    x, src, dst, edge_attr_16, edge_attr_64 = _rec_inputs()

    def _L0_gnn_setup():
        import jax, jax.numpy as jnp
        import numpy as np
        N = 12500
        E = 62500
        NUM_RADIAL = 16
        INT_EMB = 64
        HIDDEN = 128
        key = jax.random.key(seed)
        k1, k2, k3, k4, k5, k6, k7 = jax.random.split(key, 7)
        x = jax.random.normal(k1, (N, HIDDEN), dtype=jnp.float32)
        edge_index = jax.random.randint(k2, (2, E), 0, N, dtype=jnp.int64)
        edge_attr = jax.random.normal(k3, (E, NUM_RADIAL), dtype=jnp.float32)
        s1 = 1.0 / np.sqrt(NUM_RADIAL)
        s2 = 1.0 / np.sqrt(INT_EMB)
        W_emb = jax.random.uniform(k4, (NUM_RADIAL, INT_EMB), jnp.float32, -s1, s1)
        b_emb = jax.random.uniform(k5, (INT_EMB,), jnp.float32, -s1, s1)
        W_lin = jax.random.uniform(k6, (INT_EMB, HIDDEN), jnp.float32, -s2, s2)
        b_lin = jax.random.uniform(k7, (HIDDEN,), jnp.float32, -s2, s2)
        return {'x': x, 'edge_index': edge_index, 'edge_attr': edge_attr, 'W_emb': W_emb, 'b_emb': b_emb, 'W_lin': W_lin, 'b_lin': b_lin}
    _L0_gnn_all = _L0_gnn_setup()
    _L0_gnn_in = {k: v for k, v in _L0_gnn_all.items() if k in ('W_emb', 'b_emb', 'W_lin', 'b_lin')}
    del _L0_gnn_all

    def _L1_gnn_setup():
        import jax, jax.numpy as jnp
        import numpy as np
        N_NODES = 2500
        N_EDGES = 80000
        D_NODE = 128
        D_EDGE = 64
        D_OUT = 128
        key = jax.random.key(seed)
        ks = jax.random.split(key, 7)
        feats_node = jax.random.normal(ks[0], (N_NODES, D_NODE), dtype=jnp.float32)
        feats_edge = jax.random.normal(ks[1], (N_EDGES, D_EDGE), dtype=jnp.float32)
        Wn = 0.5 * jax.random.normal(ks[2], (D_OUT, D_NODE), dtype=jnp.float32)
        We = 0.5 * jax.random.normal(ks[3], (D_OUT, D_EDGE), dtype=jnp.float32)
        Wa = 0.5 * jax.random.normal(ks[4], (1, 3 * D_OUT), dtype=jnp.float32)
        src = jax.random.randint(ks[5], (N_EDGES,), 0, N_NODES, dtype=jnp.int32)
        dst = jax.random.randint(ks[6], (N_EDGES,), 0, N_NODES, dtype=jnp.int32)
        return {'feats_node': feats_node, 'feats_edge': feats_edge, 'Wn': Wn, 'We': We, 'Wa': Wa, 'src': src, 'dst': dst}
    _L1_gnn_all = _L1_gnn_setup()
    _L1_gnn_in = {k: v for k, v in _L1_gnn_all.items() if k in ('Wn', 'We', 'Wa')}
    del _L1_gnn_all
    return {'x': x, 'src': src, 'dst': dst, 'edge_attr_16': edge_attr_16, 'edge_attr_64': edge_attr_64, 'L0_gnn_W_emb': _L0_gnn_in['W_emb'], 'L0_gnn_b_emb': _L0_gnn_in['b_emb'], 'L0_gnn_W_lin': _L0_gnn_in['W_lin'], 'L0_gnn_b_lin': _L0_gnn_in['b_lin'], 'L1_gnn_Wn': _L1_gnn_in['Wn'], 'L1_gnn_We': _L1_gnn_in['We'], 'L1_gnn_Wa': _L1_gnn_in['Wa']}

def reference(x, src, dst, edge_attr_16, edge_attr_64, L0_gnn_W_emb, L0_gnn_b_emb, L0_gnn_W_lin, L0_gnn_b_lin, L1_gnn_Wn, L1_gnn_We, L1_gnn_Wa):
    import jax
    import jax.numpy as jnp

    def _L0_gnn_ref(x, edge_index, edge_attr, W_emb, b_emb, W_lin, b_lin):
        import jax, jax.numpy as jnp
        import numpy as np
        N = 12500
        E = 62500
        NUM_RADIAL = 16
        INT_EMB = 64
        HIDDEN = 128
        h = jax.nn.silu(edge_attr @ W_emb + b_emb)
        edge_emb = h @ W_lin + b_lin
        col = edge_index[1]
        out = jax.ops.segment_sum(edge_emb, col, num_segments=x.shape[0])
        return x + out

    def _L1_gnn_ref(feats_node, feats_edge, Wn, We, Wa, src, dst):
        import jax, jax.numpy as jnp
        import numpy as np
        N_NODES = 2500
        N_EDGES = 80000
        D_NODE = 128
        D_EDGE = 64
        D_OUT = 128
        n_nodes = feats_node.shape[0]
        d = Wn.shape[0]
        z_node = feats_node @ Wn.T
        z_edge = feats_edge @ We.T
        a_src, a_dst, a_e = (Wa[0, :d], Wa[0, d:2 * d], Wa[0, 2 * d:])
        z_src = z_node[src]
        z_dst = z_node[dst]
        logits = z_src @ a_src + z_dst @ a_dst + z_edge @ a_e
        e = jax.nn.leaky_relu(logits, negative_slope=0.2)
        m = jax.ops.segment_max(e, dst, num_segments=n_nodes)
        ex = jnp.exp(e - m[dst])
        s = jax.ops.segment_sum(ex, dst, num_segments=n_nodes)
        alpha = ex / jnp.where(s[dst] == 0, 1.0, s[dst])
        h = jax.ops.segment_sum(alpha[:, None] * z_src, dst, num_segments=n_nodes)
        return h
    edge_index = jnp.stack([src, dst])
    h = jnp.maximum(_layernorm(x, axis=-1), 0.0)
    x = x + _L0_gnn_ref(h, edge_index, edge_attr_16, L0_gnn_W_emb, L0_gnn_b_emb, L0_gnn_W_lin, L0_gnn_b_lin)
    h = jnp.maximum(_layernorm(x, axis=-1), 0.0)
    x = x + _L1_gnn_ref(h, edge_attr_64, L1_gnn_Wn, L1_gnn_We, L1_gnn_Wa, src, dst)
    return x

_drawn_inputs = setup_inputs


def setup_inputs(seed=0):
    import zlib

    import numpy as np

    out = dict(_drawn_inputs(seed))
    spreads = {}
    factors = {}
    for name, (base, spread) in spreads.items():
        noise = np.random.default_rng([zlib.crc32(name.encode()), seed]).standard_normal(out[name].shape)
        drawn = base * np.exp(spread * noise) if base else spread * noise
        out[name] = jnp.asarray(drawn.astype(out[name].dtype))
    for name, factor in factors.items():
        out[name] = (out[name] * factor).astype(out[name].dtype)
    return out
```

```python
from contextlib import ExitStack

import concourse.bass as bass
from concourse import mybir

ALU = mybir.AluOpType
ACT = mybir.ActivationFunctionType
AX = mybir.AxisListType
F32 = mybir.dt.float32
BF16 = mybir.dt.bfloat16
I32 = mybir.dt.int32

P = 128
TILES = 5
GROUP = TILES * P
W = 64
DIGITS = 5
ROWS = DIGITS + 2
PENALTY = 2.0 ** 110
FLOOR = -1.0e30
LN_EPS = 1e-5
RING = 4


def bass_gnn(nc, x, src, dst, ea16, ea64, w_emb, b_emb, w_lin, b_lin, wn, we, wa, out,
             q_part=125, x_part=125):
    n_nodes, D = x.shape
    n_edges, K16 = ea16.shape
    K64 = ea64.shape[1]
    H = w_emb.shape[1]
    n_groups = n_edges // GROUP
    q_blocks = n_groups // q_part
    x_blocks = n_nodes // x_part
    assert n_groups * GROUP == n_edges and q_part * q_blocks == n_groups and x_part * x_blocks == n_nodes
    assert n_nodes <= 8 ** DIGITS and D == P and H == K64 == W
    n_pad = -(-(n_nodes + 2 * W) // P) * P
    spare = n_nodes + W
    pad_part = n_pad // P
    most_steps = n_groups + n_nodes // W
    step_cols = -(-(most_steps + 2 * RING) // P)
    n_table = step_cols * P
    Z = D + 1
    ZC = D + 2

    pen_edge = nc.dram_tensor("pen_edge", (ROWS - 1, n_edges), BF16, kind="Internal").ap()
    pen_node = nc.dram_tensor("pen_node", (ROWS, n_pad), BF16, kind="Internal").ap()
    z_table = nc.dram_tensor("z_table", (n_nodes, Z), F32, kind="Internal").ap()
    q_table = nc.dram_tensor("q_table", (n_pad, 1), F32, kind="Internal").ap()
    h_table = nc.dram_tensor("h_table", (n_pad, D), F32, kind="Internal").ap()

    whole = ExitStack()

    def tensor(ctx, name, shape, dt=F32):
        return ctx.enter_context(nc.sbuf_tensor(name, shape, dt))

    def bank(ctx, name, cols=512, parts=P):
        return ctx.enter_context(nc.psum_tensor(name, [parts, cols], F32))

    def sem(ctx, name):
        return ctx.enter_context(nc.semaphore(name))

    with whole:
        eps = tensor(whole, "eps", [x_part, 1])
        ident = tensor(whole, "ident", [P, P])
        dst_e = tensor(whole, "dst_e", [P, q_part, q_blocks, TILES])
        src_e = tensor(whole, "src_e", [P, q_part, q_blocks, TILES], I32)
        base_f = tensor(whole, "base_f", [P, n_table])
        carry_sel = tensor(whole, "carry_sel", [P, n_table])
        step_g = tensor(whole, "step_g", [1, n_table], I32)
        step_b = tensor(whole, "step_b", [1, n_table], I32)
        n_iter = tensor(whole, "n_iter", [1, 1], I32)
        v_edge = tensor(whole, "v_edge", [P, K64])
        wn_x = tensor(whole, "wn_x", [P, D + 2])
        w_lin_x = tensor(whole, "w_lin_x", [H + 1, D])
        w_emb_x = tensor(whole, "w_emb_x", [TILES * K16 + 1, TILES * H])
        xn = tensor(whole, "xn", [x_part, x_blocks + 4, D])
        tables_done = sem(whole, "tables_done")
        waits_passed = sem(whole, "waits_passed")
        flat_src = src_e[:, :, :, :].rearrange("p q b j -> p (q b j)")
        flat_dst = dst_e[:, :, :, :].rearrange("p q b j -> p (q b j)")

        with ExitStack() as c:
            nat_dst = tensor(c, "nat_dst", [q_part, q_blocks * GROUP], I32)
            nat_src = tensor(c, "nat_src", [q_part, q_blocks * GROUP], I32)
            nat_f = tensor(c, "nat_f", [q_part, q_blocks * GROUP])
            digit_i = tensor(c, "digit_i", [q_part, q_blocks * GROUP], I32)
            digit_h = tensor(c, "digit_h", [q_part, q_blocks * GROUP], BF16)
            square_h = tensor(c, "square_h", [q_part, q_blocks * GROUP], BF16)
            sum_h = tensor(c, "sum_h", [q_part, q_blocks * GROUP], BF16)
            node_i = tensor(c, "node_i", [pad_part, P], I32)
            nd_i = tensor(c, "nd_i", [pad_part, P], I32)
            nd_f = tensor(c, "nd_f", [pad_part, P])
            nd_s = tensor(c, "nd_s", [pad_part, P])
            nd_q = tensor(c, "nd_q", [pad_part, P])
            nd_h = tensor(c, "nd_h", [pad_part, ROWS, P], BF16)
            last_sel = tensor(c, "last_sel", [P, P])
            row_col = tensor(c, "row_col", [P, 1])
            step_col = tensor(c, "step_col", [P, step_cols])
            ends = tensor(c, "ends", [P, n_groups + 1])
            starts = tensor(c, "starts", [P, n_groups + 1])
            span_f = tensor(c, "span_f", [P, n_groups])
            span_i = tensor(c, "span_i", [P, n_groups], I32)
            ones_g = tensor(c, "ones_g", [P, n_groups])
            found = tensor(c, "found", [P, n_groups])
            got = tensor(c, "got", [P, 4, step_cols])
            sb_f = tensor(c, "sb_f", [P, step_cols])
            sg_f = tensor(c, "sg_f", [P, step_cols])
            spare_f = tensor(c, "spare_f", [P, step_cols])
            wide_f = tensor(c, "wide_f", [P, n_table])
            count_i = tensor(c, "count_i", [1, 1], I32)
            zero_rows = tensor(c, "zero_rows", [P, D])
            wn_nat = tensor(c, "wn_nat", [P, D])
            wa_col = tensor(c, "wa_col", [P, 3])
            we_nat = tensor(c, "we_nat", [P, K64])
            turn = [bank(c, f"turn{i}", 1024) for i in range(2)]
            wide = bank(c, "wide", 1024)
            small = bank(c, "small")
            in_dst, in_src = sem(c, "in_dst"), sem(c, "in_src")
            in_w, in_wdiag, in_x = sem(c, "in_w"), sem(c, "in_wdiag"), sem(c, "in_x")
            p_const, p_ident, v_zero = sem(c, "p_const"), sem(c, "p_ident"), sem(c, "v_zero")
            v_nat, v_chain, t_turned, v_turned = sem(c, "v_nat"), sem(c, "v_chain"), sem(c, "t_turned"), sem(c, "v_turned")
            t_small, t_wide, v_small = sem(c, "t_small"), sem(c, "t_wide"), sem(c, "v_small")
            v_digit, a_square, d_digit, v_sum, d_sum = (sem(c, n) for n in ("v_digit", "a_square", "d_digit", "v_sum", "d_sum"))
            p_node, d_node, d_zero, v_cols = sem(c, "p_node"), sem(c, "d_node"), sem(c, "d_zero"), sem(c, "v_cols")
            block = c.enter_context(nc.Block())
            runs = q_blocks * GROUP

            @block.sync
            def _(sp):
                sp.dma_start(nat_dst[:, :], dst.rearrange("(q e) -> q e", q=q_part)).then_inc(in_dst, 16)
                sp.dma_start(nat_src[:, :], src.rearrange("(q e) -> q e", q=q_part)).then_inc(in_src, 16)
                sp.dma_start(xn[:, 0:x_blocks, :], x.rearrange("(p b) d -> p b d", p=x_part)).then_inc(in_x, 16)
                sp.wait_ge(v_zero, 2)
                for j in range(TILES):
                    sp.dma_start(w_emb_x[j * K16:(j + 1) * K16, j * H:(j + 1) * H], w_emb).then_inc(in_wdiag, 16)
                    sp.dma_start(w_emb_x[TILES * K16:TILES * K16 + 1, j * H:(j + 1) * H],
                                 b_emb.rearrange("(a n) -> a n", a=1)).then_inc(in_wdiag, 16)
                sp.dma_start(h_table.rearrange("(p r) d -> p r d", p=P),
                             zero_rows[:, :].unsqueeze(1).to_broadcast([P, pad_part, D])).then_inc(d_zero, 16)
                for k in range(DIGITS):
                    sp.wait_ge(v_digit, 2 * k + 2)
                    sp.dma_start(pen_edge[1 + k].rearrange("(q e) -> q e", q=q_part), digit_h[:, :]).then_inc(d_digit, 16)
                sp.wait_ge(v_sum, DIGITS)
                sp.dma_start(pen_edge[0].rearrange("(q e) -> q e", q=q_part), sum_h[:, :]).then_inc(d_sum, 16)
                sp.wait_ge(p_node, 1)
                for k in range(ROWS):
                    sp.dma_start(pen_node[k].rearrange("(p r) -> p r", r=P), nd_h[:, k, :]).then_inc(d_node, 16)
                sp.wait_ge(in_wdiag, 16 * 2 * TILES)
                sp.wait_ge(d_zero, 16)
                sp.wait_ge(d_digit, 16 * DIGITS)
                sp.wait_ge(d_sum, 16)
                sp.wait_ge(d_node, 16 * ROWS)
                sp.wait_ge(in_x, 16)

            @block.gpsimd
            def _(pool):
                pool.memset(ident[:, :], 0.0).then_inc(p_ident, 1)
                pool.memset(last_sel[:, :], 0.0).then_inc(p_ident, 1)
                pool.wait_ge(p_ident, 2)
                pool.affine_select(out=ident[:, :], in_=ident[:, :], compare_op=ALU.not_equal, fill=1.0, base=0,
                                   pattern=[[-1, P]], channel_multiplier=1).then_inc(p_const, 1)
                pool.affine_select(out=last_sel[:, :], in_=last_sel[:, :], compare_op=ALU.not_equal, fill=1.0,
                                   base=1 - P, pattern=[[0, P]], channel_multiplier=1).then_inc(p_const, 1)
                pool.iota(row_col[:, :], [[0, 1]], 0, 1, allow_small_or_imprecise_dtypes=True).then_inc(p_const, 1)
                pool.iota(step_col[:, :], [[P, step_cols]], 0, 1, allow_small_or_imprecise_dtypes=True).then_inc(p_const, 1)
                pool.iota(node_i[:, :], [[1, P]], 0, P).then_inc(p_const, 1)

            @block.scalar
            def _(act):
                act.dma_start(wn_nat[:, :], wn).then_inc(in_w, 16)
                act.dma_start(we_nat[:, :], we).then_inc(in_w, 16)
                for k in range(3):
                    act.dma_start(wa_col[:, k:k + 1], wa[:, k * D:(k + 1) * D].rearrange("a d -> d a")).then_inc(in_w, 16)
                act.dma_start(w_lin_x[0:H, :], w_lin).then_inc(in_w, 16)
                act.dma_start(w_lin_x[H:H + 1, :], b_lin.rearrange("(a n) -> a n", a=1)).then_inc(in_w, 16)
                for k in range(DIGITS):
                    act.wait_ge(v_digit, 2 * k + 2)
                    if k:
                        act.wait_ge(v_sum, k)
                    act.activation(square_h[:, :], digit_h[:, :], ACT.Square).then_inc(a_square, 1)
                act.wait_ge(in_w, 112)

            @block.tensor
            def _(pe):
                pe.wait_ge(p_const, 2)
                pe.wait_ge(in_w, 112)
                pe.transpose(small[:, 0:D], wn_nat[:, :], ident[:, :])
                pe.matmul(small[:, D:D + 2], wn_nat[:, :], wa_col[:, 0:2], start=True, stop=True)
                pe.matmul(small[:, 256:256 + K64], wa_col[:, 2:3].to_broadcast([P, P]), we_nat[:, :],
                          start=True, stop=True).then_inc(t_small, 1)
                n = 0
                for t in range(2):
                    for b in range(q_blocks):
                        if b == 0:
                            pe.wait_ge(v_nat, t + 1)
                        if n >= 2:
                            pe.wait_ge(v_turned, n - 1)
                        for j in range(TILES):
                            at = j * q_part if j < 4 else 512
                            ins = pe.transpose(turn[n % 2][:, at:at + q_part],
                                               nat_f[:, b * GROUP + j:(b + 1) * GROUP:TILES],
                                               ident[0:q_part, 0:q_part])
                        ins.then_inc(t_turned, 1)
                        n += 1
                pe.wait_ge(v_turned, q_blocks)
                ends_in = dst_e[:, :, :, TILES - 1].rearrange("p q b -> p (q b)")
                for lo in range(0, n_groups, 512):
                    hi = min(lo + 512, n_groups)
                    ins = pe.matmul(wide[:, lo:hi], last_sel[:, :], ends_in[:, lo:hi], start=True, stop=True)
                ins.then_inc(t_wide, 1)
                pe.wait_ge(v_cols, 1)
                for k in range(step_cols):
                    ins = pe.matmul(wide[:, k * P:(k + 1) * P], sb_f[:, k:k + 1].to_broadcast([P, P]), ident[:, :],
                                    start=True, stop=True)
                ins.then_inc(t_wide, 1)
                for k in range(step_cols):
                    ins = pe.matmul(turn[0][:, k * P:(k + 1) * P], sg_f[:, k:k + 1].to_broadcast([P, P]), ident[:, :],
                                    start=True, stop=True)
                ins.then_inc(t_wide, 1)

            @block.vector
            def _(v):
                chain = [0]

                def then(ins):
                    chain[0] += 1
                    ins.then_inc(v_chain, 1)
                    v.wait_ge(v_chain, chain[0])

                v.memset(w_emb_x[:, :], 0.0).then_inc(v_zero, 1)
                v.memset(zero_rows[:, :], 0.0).then_inc(v_zero, 1)
                v.memset(ones_g[:, :], 1.0)
                v.memset(eps[:, :], LN_EPS)
                v.memset(ends[:, 0:1], 0.0)
                then(v.memset(starts[:, 0:1], 0.0))
                n = 0
                for t, (nat, arrived) in enumerate(((nat_dst, in_dst), (nat_src, in_src))):
                    v.wait_ge(arrived, 16)
                    if t:
                        v.wait_ge(t_turned, q_blocks)
                    v.tensor_copy(nat_f[:, :], nat[:, :]).then_inc(v_nat, 1)
                    for b in range(q_blocks):
                        v.wait_ge(t_turned, n + 1)
                        to = (dst_e, src_e)[t]
                        v.tensor_copy(to[:, :, b, 0:4].rearrange("p q j -> p j q"),
                                      turn[n % 2][:, 0:4 * q_part].rearrange("p (j q) -> p j q", j=4))
                        v.tensor_copy(to[:, :, b, 4], turn[n % 2][:, 512:512 + q_part]).then_inc(v_turned, 1)
                        n += 1
                v.wait_ge(t_small, 1)
                v.tensor_copy(wn_x[:, :], small[:, 0:D + 2])
                v.tensor_copy(v_edge[:, :], small[:, 256:256 + K64])
                v.wait_ge(t_wide, 1)
                then(v.tensor_copy(ends[:, 1:n_groups + 1], wide[:, 0:n_groups]))
                then(v.tensor_tensor(span_i[:, :], ends[:, 1:n_groups + 1], ends[:, 0:n_groups], ALU.subtract))
                then(v.tensor_scalar(span_i[:, :], span_i[:, :], 6, None, ALU.arith_shift_right))
                then(v.tensor_copy(span_f[:, :], span_i[:, :]))
                then(v.tensor_tensor_scan(starts[:, 1:n_groups + 1], span_f[:, :], ones_g[:, :], 0.0, ALU.add, ALU.add))
                then(v.tensor_scalar(count_i[:, :], starts[0:1, n_groups:n_groups + 1], float(RING - 1), None, ALU.add))
                then(v.tensor_scalar(n_iter[:, :], count_i[:, :], 2, None, ALU.arith_shift_right))
                v.wait_ge(p_const, 5)
                for k in range(step_cols):
                    s = step_col[:, k:k + 1]
                    then(v.tensor_scalar(found[:, :], starts[:, 0:n_groups], s, None, ALU.is_le))
                    then(v.tensor_reduce(got[:, 0, k:k + 1], found[:, :], AX.X, ALU.add))
                    then(v.scalar_tensor_tensor(out=found[:, :], in0=starts[:, 0:n_groups], scalar=s,
                                                in1=starts[:, 0:n_groups], op0=ALU.is_le, op1=ALU.mult))
                    then(v.tensor_reduce(got[:, 1, k:k + 1], found[:, :], AX.X, ALU.max))
                    then(v.scalar_tensor_tensor(out=found[:, :], in0=starts[:, 0:n_groups], scalar=s,
                                                in1=ends[:, 0:n_groups], op0=ALU.is_le, op1=ALU.mult))
                    then(v.tensor_reduce(got[:, 2, k:k + 1], found[:, :], AX.X, ALU.max))
                then(v.tensor_scalar(sg_f[:, :], got[:, 0, :], 1.0, None, ALU.subtract))
                then(v.tensor_tensor(got[:, 3, :], step_col[:, :], got[:, 1, :], ALU.subtract))
                then(v.scalar_tensor_tensor(out=sb_f[:, :], in0=got[:, 3, :], scalar=float(W), in1=got[:, 2, :],
                                            op0=ALU.mult, op1=ALU.add))
                then(v.tensor_scalar(spare_f[:, :], step_col[:, :], starts[:, n_groups:n_groups + 1], None, ALU.is_ge))
                then(v.tensor_scalar(got[:, 3, :], sb_f[:, :], -1.0, float(spare), ALU.mult, ALU.add))
                then(v.tensor_tensor(got[:, 3, :], got[:, 3, :], spare_f[:, :], ALU.mult))
                v.tensor_tensor(sb_f[:, :], sb_f[:, :], got[:, 3, :], ALU.add).then_inc(v_cols, 1)
                for k in range(DIGITS):
                    if k:
                        v.wait_ge(d_digit, 16 * k)
                        v.wait_ge(a_square, k)
                    v.tensor_scalar(digit_i[:, :], nat_dst[:, :], 3 * k, 7, ALU.arith_shift_right,
                                    ALU.bitwise_and).then_inc(v_digit, 1)
                    v.wait_ge(v_digit, 2 * k + 1)
                    v.tensor_copy(digit_h[:, :], digit_i[:, :]).then_inc(v_digit, 1)
                    v.wait_ge(a_square, k + 1)
                    if k == 0:
                        v.tensor_copy(sum_h[:, :], square_h[:, :]).then_inc(v_sum, 1)
                    else:
                        v.wait_ge(v_sum, k)
                        v.tensor_tensor(sum_h[:, :], sum_h[:, :], square_h[:, :], ALU.add).then_inc(v_sum, 1)
                for k in range(DIGITS):
                    then(v.tensor_scalar(nd_i[:, :], node_i[:, :], 3 * k, 7, ALU.arith_shift_right, ALU.bitwise_and))
                    then(v.tensor_copy(nd_f[:, :], nd_i[:, :]))
                    then(v.tensor_scalar(nd_h[:, 2 + k, :], nd_f[:, :], 2.0 * PENALTY, None, ALU.mult))
                    if k == 0:
                        then(v.tensor_tensor(nd_s[:, :], nd_f[:, :], nd_f[:, :], ALU.mult))
                    else:
                        then(v.tensor_tensor(nd_q[:, :], nd_f[:, :], nd_f[:, :], ALU.mult))
                        then(v.tensor_tensor(nd_s[:, :], nd_s[:, :], nd_q[:, :], ALU.add))
                then(v.memset(nd_h[:, 1, :], -PENALTY))
                v.tensor_scalar(nd_h[:, 0, :], nd_s[:, :], -PENALTY, None, ALU.mult).then_inc(p_node, 1)
                v.wait_ge(t_wide, 2)
                then(v.tensor_copy(base_f[:, :], wide[:, 0:n_table]))
                then(v.tensor_copy(step_b[:, :], base_f[0:1, :]))
                then(v.tensor_tensor(wide_f[:, 1:n_table], base_f[:, 1:n_table], base_f[:, 0:n_table - 1], ALU.subtract))
                then(v.memset(wide_f[:, 0:1], -1.0))
                then(v.tensor_scalar(carry_sel[:, :], wide_f[:, :], row_col[:, 0:1], None, ALU.is_equal))
                v.wait_ge(t_wide, 3)
                v.tensor_copy(step_g[:, :], turn[0][0:1, 0:n_table]).then_inc(tables_done, 1)
                v.wait_ge(tables_done, 1)

        KT = TILES * K16
        last_g = n_groups - 1

        def iterations(eng):
            return eng.value_load(n_iter[0:1, 0:1], min_val=-(-n_groups // RING), max_val=-(-most_steps // RING))

        def alone(eng):
            eng.sem_inc(waits_passed, 1)

        def group_of(eng, s):
            return eng.value_load(step_g[0:1, bass.ds(s, 1)], min_val=0, max_val=last_g)

        def base_of(eng, s):
            return eng.value_load(step_b[0:1, bass.ds(s, 1)], min_val=0, max_val=spare)

        with ExitStack() as layer0:
            acc = tensor(layer0, "acc", [H + 1, n_pad])
            with ExitStack() as c:
                lnx = tensor(c, "lnx", [x_part, x_blocks, 6])
                mv = tensor(c, "mv", [x_part, x_blocks, 2])
                rstd = tensor(c, "rstd", [x_part, x_blocks])
                shift = tensor(c, "shift", [x_part, x_blocks])
                spread = tensor(c, "spread", [x_part, x_blocks])
                ln_sqrt = sem(c, "ln_sqrt")
                h0 = tensor(c, "h0", [x_part, 4, D])
                ea = tensor(c, "ea", [P, RING, KT + 1])
                offs = tensor(c, "offs", [P, RING, TILES])
                cols = tensor(c, "cols", [P, TILES, W])
                hot = tensor(c, "hot", [P, 2, TILES, W])
                ea_t = tensor(c, "ea_t", [KT + 1, 2, P])
                hid = tensor(c, "hid", [P, 2, TILES, H + 1])
                ps_t = [bank(c, f"ps_t{i}") for i in range(2)]
                ps_u = [bank(c, f"ps_u{i}") for i in range(2)]
                ps_s = [bank(c, f"ps_s{i}") for i in range(2)]
                ea_in = [sem(c, f"ea_in{u}") for u in range(RING)]
                const0, zeroed = sem(c, "const0"), sem(c, "zeroed")
                turned, copied, embedded, activated, summed, added = (
                    sem(c, n) for n in ("turned", "copied", "embedded", "activated", "summed", "added"))
                offset_set, hot_set = sem(c, "offset_set"), sem(c, "hot_set")
                ln_stat, ln_chain, ln_scale, ln_act, ln_add = (
                    sem(c, n) for n in ("ln_stat", "ln_chain", "ln_scale", "ln_act", "ln_add"))
                block = c.enter_context(nc.Block())
                ea_v = ea16.rearrange("(g p j) k -> g p (j k)", p=P, j=TILES)

                @block.sync
                def _(sp):
                    sp.wait_ge(const0, 3)
                    n = iterations(sp)

                    def load(s, u):
                        g = group_of(sp, s)
                        sp.dma_start(ea[:, u, 0:KT], ea_v[bass.ds(g, 1)].rearrange("a p k -> (a p) k")).then_inc(ea_in[u], 16)

                    for u in range(RING):
                        load(u, u)
                    with sp.Fori(0, n) as i:
                        for u in range(RING):
                            sp.wait_ge(turned, i * RING + (u + 1))
                            alone(sp)
                            load(i * RING + (u + RING), u)
                    for u in range(RING):
                        sp.wait_ge(ea_in[u], n * 16 + 16)
                        alone(sp)

                @block.gpsimd
                def _(pool):
                    pool.iota(cols[:, :, :], [[0, TILES], [1, W]], 0, 0, allow_small_or_imprecise_dtypes=True).then_inc(const0, 1)
                    n = iterations(pool)

                    def offset(s, u):
                        g = group_of(pool, s)
                        pool.tensor_tensor(offs[:, u, :], flat_dst[:, bass.ds(g * TILES, TILES)],
                                           base_f[:, bass.ds(s, 1)].to_broadcast([P, TILES]), ALU.subtract).then_inc(offset_set, 1)

                    for u in range(RING):
                        offset(u, u)
                    with pool.Fori(0, n) as i:
                        for u in range(RING):
                            pool.wait_ge(hot_set, i * RING + (u + 1))
                            offset(i * RING + (u + RING), u)
                    for b in range(x_blocks):
                        pool.wait_ge(ln_act, b + 1)
                        pool.tensor_tensor(xn[:, b, :], xn[:, b, :], h0[:, b % 4, :], ALU.add).then_inc(ln_add, 1)

                @block.scalar
                def _(act):
                    n = iterations(act)

                    def copy_t(s, u):
                        act.wait_ge(turned, s + 1)
                        act.activation(ea_t[:, u % 2, :], ps_t[u % 2][0:KT + 1, 0:P], ACT.Copy).then_inc(copied, 1)

                    def silu(s, u):
                        act.wait_ge(embedded, s + 1)
                        act.activation(hid[:, u % 2, :, 0:H], ps_u[u % 2][:, 0:TILES * H].rearrange("p (j h) -> p j h", j=TILES),
                                       ACT.Silu).then_inc(activated, 1)

                    act.wait_ge(ln_chain, x_blocks)
                    act.activation(spread[:, :], mv[:, :, 1], ACT.Sqrt, bias=eps[:, :]).then_inc(ln_sqrt, 1)
                    act.wait_ge(const0, 3)
                    copy_t(0, 0)
                    copy_t(1, 1)
                    silu(0, 0)
                    with act.Fori(0, n) as i:
                        for u in range(RING):
                            s = i * RING + u
                            act.wait_ge(embedded, s + 1)
                            copy_t(s + 2, u)
                            act.wait_ge(summed, s + 1)
                            silu(s + 1, u + 1)
                    act.wait_ge(ln_scale, 1)
                    for b in range(x_blocks):
                        if b >= 4:
                            act.wait_ge(ln_add, b - 3)
                        act.activation(h0[:, b % 4, :], xn[:, b, :], ACT.Relu, bias=shift[:, b:b + 1],
                                       scale=rstd[:, b:b + 1]).then_inc(ln_act, 1)

                @block.tensor
                def _(pe):
                    n = iterations(pe)
                    pe.sem_inc(summed, 1)

                    def turn_edges(s, u):
                        pe.transpose(ps_t[u % 2][0:KT + 1, 0:P], ea[:, u % RING, :], ident[:, :]).then_inc(turned, 1)

                    def embed(s, u):
                        pe.wait_ge(copied, s + 1)
                        pe.matmul(ps_u[u % 2][:, 0:TILES * H], ea_t[:, u % 2, :], w_emb_x[:, :], start=True,
                                  stop=True).then_inc(embedded, 1)

                    def sum_up(s, u):
                        pe.wait_ge(activated, s + 1)
                        pe.wait_ge(hot_set, s + 1)
                        pe.wait_ge(added, s + 1)
                        for j in range(TILES):
                            ins = pe.matmul(ps_s[u % 2][0:H + 1, 0:W], hid[:, u % 2, j, :], hot[:, u % 2, j, :],
                                            start=(j == 0), stop=(j == TILES - 1))
                        ins.then_inc(summed, 1)

                    pe.wait_ge(const0, 3)
                    pe.wait_ge(ea_in[0], 16)
                    turn_edges(0, 0)
                    pe.wait_ge(ea_in[1], 16)
                    turn_edges(1, 1)
                    embed(0, 0)
                    with pe.Fori(0, n) as i:
                        for u in range(RING):
                            s = i * RING + u
                            pe.wait_ge(ea_in[(u + 2) % RING], i * 16 + 16 * (1 + (u + 2) // RING))
                            pe.wait_ge(copied, s + 1)
                            turn_edges(s + 2, u + 2)
                            embed(s + 1, u + 1)
                            sum_up(s, u)

                @block.vector
                def _(v):
                    v.sem_inc(added, 2)
                    v.memset(ea[:, :, KT:KT + 1], 1.0).then_inc(const0, 1)
                    v.memset(hid[:, :, :, H:H + 1], 1.0).then_inc(const0, 1)
                    v.memset(xn[:, x_blocks:x_blocks + 4, :], 0.0)
                    v.memset(acc[:, :], 0.0).then_inc(zeroed, 1)
                    for b in range(x_blocks):
                        v.bn_stats(lnx[:, b, :], xn[:, b, :]).then_inc(ln_stat, 1)
                    for b in range(x_blocks):
                        v.wait_ge(ln_stat, b + 1)
                        v.bn_aggr(mv[:, b, :], lnx[:, b, :]).then_inc(ln_chain, 1)
                    v.wait_ge(ln_chain, x_blocks)
                    v.wait_ge(ln_sqrt, 1)
                    v.reciprocal(rstd[:, :], spread[:, :]).then_inc(ln_chain, 1)
                    v.wait_ge(ln_chain, x_blocks + 1)
                    v.scalar_tensor_tensor(out=shift[:, :], in0=mv[:, :, 0], scalar=-1.0, in1=rstd[:, :],
                                           op0=ALU.mult, op1=ALU.mult).then_inc(ln_scale, 1)
                    v.wait_ge(zeroed, 1)
                    v.wait_ge(const0, 3)
                    n = iterations(v)

                    def one_hot(s, u):
                        v.wait_ge(offset_set, s + 1)
                        v.tensor_tensor(hot[:, u % 2], cols[:, :, :],
                                        offs[:, u % RING, :].unsqueeze(2).to_broadcast([P, TILES, W]),
                                        ALU.is_equal).then_inc(hot_set, 1)

                    one_hot(0, 0)
                    with v.Fori(0, n) as i:
                        for u in range(RING):
                            s = i * RING + u
                            v.wait_ge(summed, s + 1)
                            one_hot(s + 1, u + 1)
                            b = base_of(v, s)
                            v.wait_ge(summed, s + 2)
                            v.wait_ge(added, s + 2)
                            v.tensor_tensor(acc[:, bass.ds(b, W)], acc[:, bass.ds(b, W)], ps_s[u % 2][0:H + 1, 0:W],
                                            ALU.add).then_inc(added, 1)

            with ExitStack() as c:
                CH = 2
                chunks = x_blocks // CH
                assert chunks % 2 == 0
                stats = tensor(c, "stats", [x_part, 2, CH, 6])
                mv = tensor(c, "mv1", [x_part, 2, CH, 2])
                rstd = tensor(c, "rstd1", [x_part, 2, CH])
                shift = tensor(c, "shift1", [x_part, 2, CH])
                spread = tensor(c, "spread1", [x_part, 2, CH])
                spread_set = sem(c, "spread_set")
                acc_n = tensor(c, "acc_n", [H + 1, 2, CH, x_part])
                h1 = tensor(c, "h1", [x_part, 2, CH, D])
                h1_t = tensor(c, "h1_t", [D, 2, CH * x_part])
                z_out = tensor(c, "z_out", [x_part, 2, CH, Z])
                q_out = tensor(c, "q_out", [x_part, x_blocks])
                q_zero = tensor(c, "q_zero", [1, n_pad - n_nodes])
                ps_x = [bank(c, f"ps_x{i}") for i in range(2)]
                ps_h = [bank(c, f"ps_h{i}") for i in range(2)]
                ps_z = [bank(c, f"ps_z{i}") for i in range(2)]
                acc_copied, x1_sum, x1_set, stat_set, mv_set, rstd_set, shift_set = (
                    sem(c, n) for n in ("acc_copied", "x1_sum", "x1_set", "stat_set", "mv_set", "rstd_set", "shift_set"))
                h1_set, h1_turned, h1_copied, z_sum, z_set, q_set = (
                    sem(c, n) for n in ("h1_set", "h1_turned", "h1_copied", "z_sum", "z_set", "q_set"))
                z_stored = [sem(c, f"z_stored{u}") for u in range(2)]
                z_free, q_stored, q_zeroed = sem(c, "z_free"), sem(c, "q_stored"), sem(c, "q_zeroed")
                block = c.enter_context(nc.Block())

                @block.sync
                def _(sp):
                    z_v = z_table.rearrange("(p b) c -> p b c", p=x_part)
                    with sp.Fori(0, chunks // 2) as i:
                        for u in range(2):
                            sp.wait_ge(z_set, i * 2 + (u + 1))
                            sp.dma_start(z_v[:, bass.ds(i * (2 * CH) + u * CH, CH), :], z_out[:, u, :, :]).then_inc(z_stored[u], 16)
                            sp.wait_ge(z_stored[u], i * 16 + 16)
                            sp.sem_inc(z_free, 1)
                    sp.wait_ge(q_set, chunks)
                    sp.wait_ge(q_zeroed, 1)
                    sp.dma_start(q_table[0:n_nodes].rearrange("(p b) c -> p (b c)", p=x_part), q_out[:, :]).then_inc(q_stored, 16)
                    sp.dma_start(q_table[n_nodes:n_pad].rearrange("n a -> a n"), q_zero[:, :]).then_inc(q_stored, 16)
                    sp.wait_ge(q_stored, 32)

                @block.scalar
                def _(act):
                    def copy_acc(b, u):
                        for k in range(CH):
                            ins = act.activation(acc_n[:, u % 2, k, :].unsqueeze(2),
                                                 acc[:, bass.ds(b + k, (x_part - 1) * x_blocks + 1)][:, 0:(x_part - 1) * x_blocks + 1:x_blocks].unsqueeze(2),
                                                 ACT.Copy)
                        ins.then_inc(acc_copied, 1)

                    def root(c0, u):
                        act.wait_ge(mv_set, c0 + 1)
                        act.activation(spread[:, u % 2, :], mv[:, u % 2, :, 1], ACT.Sqrt,
                                       bias=eps[:, :]).then_inc(spread_set, 1)

                    copy_acc(0, 0)
                    copy_acc(CH, 1)
                    root(0, 0)
                    with act.Fori(0, chunks // 2) as i:
                        for u in range(2):
                            c0 = i * 2 + u
                            act.wait_ge(shift_set, c0 + 1)
                            for k in range(CH):
                                b = c0 * CH + k
                                ins = act.activation(h1[:, u, k, :], xn[:, bass.ds(b, 1), :].rearrange("p a d -> p (a d)"), ACT.Relu,
                                                     bias=shift[:, u, k:k + 1], scale=rstd[:, u, k:k + 1])
                            ins.then_inc(h1_set, 1)
                            act.wait_ge(x1_sum, c0 + 1)
                            copy_acc(c0 * CH + 2 * CH, u)
                            root(c0 + 1, u + 1)
                            act.wait_ge(h1_turned, c0 + 1)
                            act.wait_ge(z_sum, c0 + 1)
                            act.activation(h1_t[:, u, :], ps_h[u][:, 0:CH * x_part], ACT.Copy).then_inc(h1_copied, 1)

                @block.tensor
                def _(pe):
                    pe.sem_inc(z_sum, 2)

                    def x_sum(c0, u):
                        pe.wait_ge(acc_copied, c0 + 1)
                        for k in range(CH):
                            ins = pe.matmul(ps_x[u % 2][0:x_part, k * D:(k + 1) * D], acc_n[:, u % 2, k, :], w_lin_x[:, :],
                                            start=True, stop=True)
                        ins.then_inc(x1_sum, 1)

                    x_sum(0, 0)
                    with pe.Fori(0, chunks // 2) as i:
                        for u in range(2):
                            c0 = i * 2 + u
                            pe.wait_ge(h1_set, c0 + 1)
                            for k in range(CH):
                                ins = pe.transpose(ps_h[u][:, k * x_part:(k + 1) * x_part], h1[:, u, k, :],
                                                   ident[0:x_part, 0:x_part])
                            ins.then_inc(h1_turned, 1)
                            x_sum(c0 + 1, u + 1)
                            pe.wait_ge(h1_copied, c0 + 1)
                            for k in range(CH):
                                ins = pe.matmul(ps_z[u][0:x_part, k * (D + 2):(k + 1) * (D + 2)],
                                                h1_t[:, u, k * x_part:(k + 1) * x_part], wn_x[:, :], start=True, stop=True)
                            ins.then_inc(z_sum, 1)

                @block.vector
                def _(v):
                    v.memset(q_zero[:, :], 0.0).then_inc(q_zeroed, 1)
                    v.sem_inc(z_free, 2)

                    def x_one(c0, u):
                        b = c0 * CH
                        v.wait_ge(x1_sum, c0 + 1)
                        xs = xn[:, bass.ds(b, CH), :]
                        v.tensor_tensor(xs, xs, ps_x[u % 2][0:x_part, 0:CH * D].rearrange("p (k d) -> p k d", k=CH),
                                        ALU.add).then_inc(x1_set, 1)
                        v.wait_ge(x1_set, c0 + 1)
                        alone(v)
                        for k in range(CH):
                            ins = v.bn_stats(stats[:, u % 2, k, :],
                                             xn[:, bass.ds(b + k, 1), :].rearrange("p a d -> p (a d)"))
                        ins.then_inc(stat_set, 1)
                        v.wait_ge(stat_set, c0 + 1)
                        alone(v)
                        for k in range(CH):
                            ins = v.bn_aggr(mv[:, u % 2, k, :], stats[:, u % 2, k, :])
                        ins.then_inc(mv_set, 1)
                        v.wait_ge(spread_set, c0 + 1)
                        v.reciprocal(rstd[:, u % 2, :], spread[:, u % 2, :]).then_inc(rstd_set, 1)
                        v.wait_ge(rstd_set, c0 + 1)
                        v.scalar_tensor_tensor(out=shift[:, u % 2, :], in0=mv[:, u % 2, :, 0], scalar=-1.0,
                                               in1=rstd[:, u % 2, :], op0=ALU.mult, op1=ALU.mult).then_inc(shift_set, 1)

                    x_one(0, 0)
                    with v.Fori(0, chunks // 2) as i:
                        for u in range(2):
                            c0 = i * 2 + u
                            x_one(c0 + 1, u + 1)
                            v.wait_ge(z_free, c0 + 1)
                            v.wait_ge(z_sum, c0 + 3)
                            z = ps_z[u][0:x_part, 0:CH * (D + 2)].rearrange("p (k d) -> p k d", k=CH)
                            v.tensor_copy(z_out[:, u, :, :], z[:, :, 0:Z]).then_inc(z_set, 1)
                            v.tensor_copy(q_out[:, bass.ds(c0 * CH, CH)], z[:, :, D + 1]).then_inc(q_set, 1)

        with ExitStack() as c:
            edge_f = tensor(c, "edge_f", [P, RING, TILES, K64])
            index = tensor(c, "index", [P, RING, TILES], I32)
            rows = tensor(c, "rows", [P, RING, TILES, ZC])
            pen_e = tensor(c, "pen_e", [ROWS, RING, GROUP], BF16)
            pen_n = tensor(c, "pen_n", [ROWS, RING, W], BF16)
            q_win = tensor(c, "q_win", [W, RING])
            sel = tensor(c, "sel", [W, RING])
            product = tensor(c, "product", [P, TILES, K64])
            edge_r = tensor(c, "edge_r", [P, TILES])
            logit = tensor(c, "logit", [P, TILES])
            top = tensor(c, "top", [W, 1])
            top_q = tensor(c, "top_q", [W, 1])
            top_l = tensor(c, "top_l", [W, 1])
            peak = tensor(c, "peak", [W, 2])
            carried = tensor(c, "carried", [W, 1])
            bias1 = tensor(c, "bias1", [W, 1])
            bias2 = tensor(c, "bias2", [W, 1])
            valid = tensor(c, "valid", [1, 1])
            fade = tensor(c, "fade", [1, 2])
            prob1 = tensor(c, "prob1", [W, GROUP])
            prob2 = tensor(c, "prob2", [W, GROUP])
            prob_t = tensor(c, "prob_t", [P, TILES, W])
            prob_a = tensor(c, "prob_a", [P, TILES * W])
            row0 = tensor(c, "row0", [1, W])
            carry_in = tensor(c, "carry_in", [1, ZC])
            total = tensor(c, "total", [W, ZC])
            weight = tensor(c, "weight", [W, 1])
            inverse = tensor(c, "inverse", [W, 1])
            h_out = tensor(c, "h_out", [W, 2, D])
            ps_m = bank(c, "ps_m", 1024, W)
            ps_p1 = bank(c, "ps_p1")
            ps_p2 = bank(c, "ps_p2")
            ps_o = bank(c, "ps_o")
            ps_cm = bank(c, "ps_cm")
            ps_ca = bank(c, "ps_ca")
            const1 = sem(c, "const1")
            index_in = [sem(c, f"index_in{u}") for u in range(RING)]
            loads_in = [sem(c, f"loads_in{u}") for u in range(RING)]
            rows_in = [sem(c, f"rows_in{u}") for u in range(RING)]
            product_set, r_set, logit_set, scored, top_set, topq_set, topl_set, peak_set, bias1_set, bias2_set = (
                sem(c, n) for n in ("product_set", "r_set", "logit_set", "scored", "top_set", "topq_set", "topl_set",
                                    "peak_set", "bias1_set", "bias2_set"))
            peak_carried, valid_set, carried_set, fade_set, prob_set, prob_turned, prob_t_set = (
                sem(c, n) for n in ("peak_carried", "valid_set", "carried_set", "fade_set", "prob_set", "prob_turned",
                                    "prob_t_set"))
            total_carried, carry_set, summed, total_set, weight_set, inverse_set, h_set, h_free = (
                sem(c, n) for n in ("total_carried", "carry_set", "summed1", "total_set", "weight_set", "inverse_set",
                                    "h_set", "h_free"))
            prob_copied = sem(c, "prob_copied")
            h_stored = [sem(c, f"h_stored{u}") for u in range(2)]
            CONSTS = 6
            block = c.enter_context(nc.Block())
            ea_v = ea64.rearrange("(g p j) k -> g p (j k)", p=P, j=TILES)

            @block.sync
            def _(sp):
                sp.wait_ge(const1, CONSTS)
                n = iterations(sp)

                def load(s, u):
                    g = group_of(sp, s)
                    b = base_of(sp, s)
                    sp.dma_start(index[:, u, :], flat_src[:, bass.ds(g * TILES, TILES)]).then_inc(index_in[u], 16)
                    for to, of in ((edge_f[:, u, :, :].rearrange("p j k -> p (j k)"), ea_v[bass.ds(g, 1)].rearrange("a p k -> (a p) k")),
                                   (pen_e[1:ROWS, u, :], pen_edge[:, bass.ds(g * GROUP, GROUP)]),
                                   (pen_n[:, u, :], pen_node[:, bass.ds(b, W)]),
                                   (q_win[:, u:u + 1], q_table[bass.ds(b, W), :]),
                                   (sel[:, u:u + 1], carry_sel[0:W, bass.ds(s, 1)])):
                        sp.dma_start(to, of).then_inc(loads_in[u], 16)

                for u in range(RING):
                    load(u, u)
                sp.dma_start(h_table[spare:spare + W, :], h_out[:, 1, :]).then_inc(h_stored[1], 16)
                with sp.Fori(0, n) as i:
                    for u in range(RING):
                        s = i * RING + u
                        sp.wait_ge(summed, s + 1)
                        alone(sp)
                        load(s + RING, u)
                        b = base_of(sp, s)
                        sp.wait_ge(h_set, s + 1)
                        alone(sp)
                        sp.wait_ge(h_stored[(u + 1) % 2], i * 32 + 16 * (1 + u // 2))
                        sp.sem_inc(h_free, 1)
                        sp.dma_start(h_table[bass.ds(b, W), :], h_out[:, u % 2, :]).then_inc(h_stored[u % 2], 16)
                for u in range(RING):
                    sp.wait_ge(index_in[u], n * 16 + 16)
                    sp.wait_ge(loads_in[u], n * 80 + 80)
                sp.wait_ge(h_stored[1], n * 32 + 16)
                sp.wait_ge(h_stored[0], n * 32)
                alone(sp)

            @block.gpsimd
            def _(pool):
                n = iterations(pool)

                def gather(u, count):
                    pool.wait_ge(index_in[u], count)
                    alone(pool)
                    for j in range(TILES):
                        pool.indirect_dma_start(rows[:, u, j, 0:Z], None, z_table,
                                                bass.IndirectOffsetOnAxis(ap=index[:, u, j:j + 1], axis=0)).then_inc(rows_in[u], 16)

                pool.wait_ge(const1, CONSTS)
                gather(0, 16)
                with pool.Fori(0, n) as i:
                    for u in range(RING):
                        gather((u + 1) % RING, i * 16 + 16 * (1 + (u + 1) // RING))

            @block.scalar
            def _(act):
                n = iterations(act)

                def exps(s, u):
                    act.wait_ge(bias2_set, s + 1)
                    act.activation(fade[:, u % 2:u % 2 + 1], peak[0:1, 0:1], ACT.Exp, bias=carried[0:1, :], scale=-1.0).then_inc(fade_set, 1)
                    act.activation(prob1[:, :], ps_m[:, 0:GROUP], ACT.Exp, bias=bias1[:, :])
                    act.activation(prob2[:, :], ps_m[:, 0:GROUP], ACT.Exp, bias=bias2[:, :], scale=0.2).then_inc(prob_set, 1)

                exps(0, 0)
                with act.Fori(0, n) as i:
                    for u in range(RING):
                        s = i * RING + u
                        act.wait_ge(prob_turned, s * 2 + 1)
                        act.activation(prob_a[:, :], ps_p1[:, 0:TILES * W], ACT.Copy).then_inc(prob_copied, 1)
                        act.wait_ge(total_carried, s + 1)
                        act.wait_ge(fade_set, s + 1)
                        act.activation(carry_in[:, :], ps_ca[0:1, 0:ZC], ACT.Copy, scale=fade[0:1, u % 2:u % 2 + 1]).then_inc(carry_set, 1)
                        exps(s + 1, u + 1)

            @block.tensor
            def _(pe):
                n = iterations(pe)

                def score(s, u, count):
                    pe.wait_ge(loads_in[u], count)
                    pe.wait_ge(logit_set, s + 1)
                    for lo, hi in ((0, 4), (4, 5)):
                        e = pen_e[:, u, :].rearrange("r (p j) -> r j p", j=TILES)[:, lo:hi, :]
                        pe.matmul(ps_m[:, lo * P:hi * P], pen_n[:, u, :], e, start=True, stop=False)
                    for j in range(TILES):
                        ins = pe.matmul(ps_m[:, j * P:(j + 1) * P], logit[:, j:j + 1].to_broadcast([P, W]), ident[:, :],
                                        start=False, stop=(j >= 3))
                    ins.then_inc(scored, 1)

                def carry_peak(s, u):
                    pe.wait_ge(peak_set, s)
                    alone(pe)
                    pe.matmul(ps_cm[0:1, 0:2], sel[:, u:u + 1], peak[:, :], start=True, stop=True).then_inc(peak_carried, 1)

                pe.wait_ge(const1, CONSTS)
                pe.wait_ge(loads_in[0], 80)
                pe.matmul(ps_cm[0:1, 0:2], sel[:, 0:1], peak[:, :], start=True, stop=True).then_inc(peak_carried, 1)
                score(0, 0, 80)
                with pe.Fori(0, n) as i:
                    for u in range(RING):
                        s = i * RING + u
                        u1 = (u + 1) % RING
                        pe.wait_ge(loads_in[u1], i * 80 + 80 * (1 + (u + 1) // RING))
                        carry_peak(s + 1, u1)
                        pe.wait_ge(total_set, s + 1)
                        alone(pe)
                        pe.matmul(ps_ca[0:1, 0:ZC], sel[:, u:u + 1], total[:, :], start=True, stop=True).then_inc(total_carried, 1)
                        pe.wait_ge(prob_set, s + 1)
                        alone(pe)
                        for prob, ps in ((prob1, ps_p1), (prob2, ps_p2)):
                            for j in range(TILES):
                                ins = pe.transpose(ps[:, j * W:(j + 1) * W], prob[:, j * P:(j + 1) * P], ident[0:W, 0:W])
                            ins.then_inc(prob_turned, 1)
                        score(s + 1, u1, i * 80 + 80 * (1 + (u + 1) // RING))
                        pe.wait_ge(carry_set, s + 1)
                        pe.wait_ge(prob_t_set, s + 1)
                        for j in range(TILES):
                            pe.matmul(ps_o[0:W, 0:ZC], prob_t[:, j, :], rows[:, u, j, :], start=(j == 0), stop=False)
                        pe.matmul(ps_o[0:W, 0:ZC], row0[:, :], carry_in[:, :], start=False, stop=True).then_inc(summed, 1)

            @block.vector
            def _(v):
                v.sem_inc(total_set, 1)
                v.sem_inc(h_free, 1)
                v.memset(rows[:, :, :, Z:ZC], 1.0).then_inc(const1, 1)
                v.memset(pen_e[0:1, :, :], 1.0).then_inc(const1, 1)
                v.memset(peak[:, :], 1.0).then_inc(const1, 1)
                v.memset(carried[:, :], FLOOR)
                v.memset(total[:, :], 0.0).then_inc(const1, 1)
                v.memset(h_out[:, :, :], 0.0).then_inc(const1, 1)
                v.tensor_copy(row0[:, :], ident[0:1, 0:W]).then_inc(const1, 1)
                v.wait_ge(const1, CONSTS)
                n = iterations(v)

                def logits(s, u, loads, gathered):
                    v.wait_ge(loads_in[u], loads)
                    v.tensor_tensor(product[:, :, :], edge_f[:, u, :, :],
                                    v_edge[:, :].unsqueeze(1).to_broadcast([P, TILES, K64]), ALU.mult).then_inc(product_set, 1)
                    v.wait_ge(product_set, s + 1)
                    v.tensor_reduce(edge_r[:, :], product[:, :, :], AX.X, ALU.add).then_inc(r_set, 1)
                    v.wait_ge(r_set, s + 1)
                    v.wait_ge(rows_in[u], gathered)
                    v.tensor_tensor(logit[:, :], edge_r[:, :], rows[:, u, :, D], ALU.add).then_inc(logit_set, 1)

                def peaks(s, u):
                    v.wait_ge(peak_carried, s + 1)
                    v.tensor_scalar(valid[:, :], ps_cm[0:1, 1:2], 1.0, -FLOOR, ALU.subtract, ALU.mult).then_inc(valid_set, 1)
                    v.wait_ge(valid_set, s + 1)
                    v.tensor_tensor(carried[0:1, :], valid[:, :], ps_cm[0:1, 0:1], ALU.add).then_inc(carried_set, 1)
                    v.wait_ge(scored, s + 1)
                    v.tensor_reduce(top[:, :], ps_m[:, 0:GROUP], AX.X, ALU.max).then_inc(top_set, 1)
                    v.wait_ge(top_set, s + 1)
                    q = q_win[:, u:u + 1]
                    v.tensor_tensor(top_q[:, :], top[:, :], q, ALU.add).then_inc(topq_set, 1)
                    v.wait_ge(topq_set, s + 1)
                    v.scalar_tensor_tensor(out=top_l[:, :], in0=top_q[:, :], scalar=0.2, in1=top_q[:, :], op0=ALU.mult,
                                           op1=ALU.max).then_inc(topl_set, 1)
                    v.wait_ge(topl_set, s + 1)
                    v.wait_ge(carried_set, s + 1)
                    v.tensor_tensor(peak[:, 0:1], top_l[:, :], carried[:, :], ALU.max).then_inc(peak_set, 1)
                    v.wait_ge(peak_set, s + 1)
                    v.tensor_tensor(bias1[:, :], q, peak[:, 0:1], ALU.subtract).then_inc(bias1_set, 1)
                    v.scalar_tensor_tensor(out=bias2[:, :], in0=q, scalar=0.2, in1=peak[:, 0:1], op0=ALU.mult,
                                           op1=ALU.subtract).then_inc(bias2_set, 1)

                logits(0, 0, 80, 80)
                peaks(0, 0)
                with v.Fori(0, n) as i:
                    for u in range(RING):
                        s = i * RING + u
                        u1 = (u + 1) % RING
                        count = i * 80 + 80 * (1 + (u + 1) // RING)
                        logits(s + 1, u1, count, count)
                        v.wait_ge(prob_turned, s * 2 + 2)
                        v.wait_ge(prob_copied, s + 1)
                        v.tensor_tensor(prob_t[:, :, :].rearrange("p j w -> p (j w)"), prob_a[:, :],
                                        ps_p2[:, 0:TILES * W], ALU.max).then_inc(prob_t_set, 1)
                        peaks(s + 1, u1)
                        v.wait_ge(summed, s + 1)
                        v.tensor_copy(total[:, :], ps_o[0:W, 0:ZC]).then_inc(total_set, 1)
                        v.wait_ge(total_set, s + 2)
                        s_col = total[:, ZC - 1:ZC]
                        v.scalar_tensor_tensor(out=weight[:, :], in0=s_col, scalar=0.0, in1=s_col, op0=ALU.is_equal,
                                               op1=ALU.add).then_inc(weight_set, 1)
                        v.wait_ge(weight_set, s + 1)
                        v.reciprocal(inverse[:, :], weight[:, :]).then_inc(inverse_set, 1)
                        v.wait_ge(inverse_set, s + 1)
                        v.wait_ge(h_free, s + 1)
                        v.tensor_scalar(h_out[:, u % 2, :], total[:, 0:D], inverse[:, 0:1], None, ALU.mult).then_inc(h_set, 1)

        with ExitStack() as c:
            step = max(1, x_blocks // 10)
            parts = x_blocks // step
            h_in = tensor(c, "h_in", [x_part, x_blocks, D])
            h_loaded = [sem(c, f"h_loaded{t}") for t in range(parts)]
            out_set, out_stored = sem(c, "out_set"), sem(c, "out_stored")
            block = c.enter_context(nc.Block())

            @block.sync
            def _(sp):
                h_v = h_table[0:n_nodes].rearrange("(p b) d -> p b d", p=x_part)
                for t in range(parts):
                    sp.dma_start(h_in[:, t * step:(t + 1) * step, :], h_v[:, t * step:(t + 1) * step, :]).then_inc(h_loaded[t], 16)

            @block.vector
            def _(v):
                for t in range(parts):
                    v.wait_ge(h_loaded[t], 16)
                    h = h_in[:, t * step:(t + 1) * step, :]
                    v.tensor_tensor(h, h, xn[:, t * step:(t + 1) * step, :], ALU.add).then_inc(out_set, 1)

            @block.scalar
            def _(act):
                o_v = out.rearrange("(p b) d -> p b d", p=x_part)
                for t in range(parts):
                    act.wait_ge(out_set, t + 1)
                    act.dma_start(o_v[:, t * step:(t + 1) * step, :], h_in[:, t * step:(t + 1) * step, :]).then_inc(out_stored, 16)
                act.wait_ge(out_stored, 16 * parts)


_INS = ["x", "src", "dst", "edge_attr_16", "edge_attr_64", "L0_gnn_W_emb", "L0_gnn_b_emb", "L0_gnn_W_lin", "L0_gnn_b_lin",
        "L1_gnn_Wn", "L1_gnn_We", "L1_gnn_Wa"]


def kernel(**inputs):
    import numpy as np
    import concourse.bacc as bacc
    from concourse.bass_utils import run_bass_kernel_spmd

    nc = bacc.Bacc("TRN2", target_bir_lowering=False, num_devices=1)
    arrays, args = {}, []
    for name in _INS:
        a = np.ascontiguousarray(inputs[name])
        arrays[f"in_{name}"] = a
        args.append(nc.dram_tensor(f"in_{name}", a.shape, mybir.dt.from_np(a.dtype), kind="ExternalInput").ap())
    out = nc.dram_tensor("out_0", arrays["in_x"].shape, F32, kind="ExternalOutput").ap()
    bass_gnn(nc, *args, out)
    r = run_bass_kernel_spmd(nc, [arrays], core_ids=[0])
    return r.results[0]["out_0"]
```

```python
from contextlib import ExitStack

import concourse.bass as bass
from concourse import mybir

ALU = mybir.AluOpType
ACT = mybir.ActivationFunctionType
AX = mybir.AxisListType
F32 = mybir.dt.float32
BF16 = mybir.dt.bfloat16
I32 = mybir.dt.int32

P = 128
TILES = 5
GROUP = TILES * P
W = 64
DIGITS = 5
NODE_BITS = 14
ROWS = DIGITS + 2
PENALTY = 2.0 ** 110
FLOOR = -1.0e30
LN_EPS = 1e-5
HALF = 3
RING = 2 * HALF


def bass_gnn(nc, x, src, dst, ea16, ea64, w_emb, b_emb, w_lin, b_lin, wn, we, wa, out,
             q_part=125, x_part=125):
    n_nodes, D = x.shape
    n_edges, K16 = ea16.shape
    K64 = ea64.shape[1]
    H = w_emb.shape[1]
    n_groups = n_edges // GROUP
    q_blocks = n_groups // q_part
    x_blocks = n_nodes // x_part
    assert n_groups * GROUP == n_edges and q_part * q_blocks == n_groups and x_part * x_blocks == n_nodes
    assert n_nodes <= 8 ** DIGITS and n_nodes + W < 2 ** NODE_BITS and n_groups * 2 ** NODE_BITS <= 2 ** 24 and D == P and H == K64 == W
    n_pad = -(-(n_nodes + 2 * W) // P) * P
    spare = n_nodes + W
    pad_part = n_pad // P
    most_steps = n_groups + n_nodes // W
    most_iter = -(-most_steps // RING)
    step_cols = -(-(most_iter * RING + RING) // P)
    n_table = step_cols * P
    Z = D + 1
    ZC = D + 2

    pen_edge = nc.dram_tensor("pen_edge", (ROWS - 1, n_edges), BF16, kind="Internal").ap()
    pen_node = nc.dram_tensor("pen_node", (ROWS, n_pad), BF16, kind="Internal").ap()
    z_table = nc.dram_tensor("z_table", (n_nodes, Z), F32, kind="Internal").ap()
    q_table = nc.dram_tensor("q_table", (n_pad, 1), F32, kind="Internal").ap()
    h_table = nc.dram_tensor("h_table", (n_pad, D), F32, kind="Internal").ap()

    whole = ExitStack()

    def tensor(ctx, name, shape, dt=F32):
        return ctx.enter_context(nc.sbuf_tensor(name, shape, dt))

    def bank(ctx, name, cols=512, parts=P):
        return ctx.enter_context(nc.psum_tensor(name, [parts, cols], F32))

    def sem(ctx, name):
        return ctx.enter_context(nc.semaphore(name))

    with whole:
        eps = tensor(whole, "eps", [x_part, 1])
        ident = tensor(whole, "ident", [P, P])
        dst_e = tensor(whole, "dst_e", [P, q_part, q_blocks, TILES])
        src_e = tensor(whole, "src_e", [P, q_part, q_blocks, TILES], I32)
        base_f = tensor(whole, "base_f", [P, n_table])
        carry_sel = tensor(whole, "carry_sel", [P, n_table])
        step_gb = tensor(whole, "step_gb", [1, n_table], I32)
        n_iter = tensor(whole, "n_iter", [1, 1], I32)
        v_edge = tensor(whole, "v_edge", [P, K64])
        wn_x = tensor(whole, "wn_x", [P, D + 2])
        w_lin_x = tensor(whole, "w_lin_x", [H + 1, D])
        w_emb_x = tensor(whole, "w_emb_x", [TILES * K16 + 1, TILES * H])
        xn = tensor(whole, "xn", [x_part, x_blocks + 4, D])
        tables_done = sem(whole, "tables_done")
        waits_passed = sem(whole, "waits_passed")
        flat_src = src_e[:, :, :, :].rearrange("p q b j -> p (q b j)")
        flat_dst = dst_e[:, :, :, :].rearrange("p q b j -> p (q b j)")

        with ExitStack() as c:
            nat_dst = tensor(c, "nat_dst", [q_part, q_blocks * GROUP], I32)
            nat_src = tensor(c, "nat_src", [q_part, q_blocks * GROUP], I32)
            nat_f = tensor(c, "nat_f", [q_part, q_blocks * GROUP])
            digit_i = tensor(c, "digit_i", [q_part, q_blocks * GROUP], I32)
            digit_h = tensor(c, "digit_h", [q_part, q_blocks * GROUP], BF16)
            square_h = tensor(c, "square_h", [q_part, q_blocks * GROUP], BF16)
            sum_h = tensor(c, "sum_h", [q_part, q_blocks * GROUP], BF16)
            node_i = tensor(c, "node_i", [pad_part, P], I32)
            nd_i = tensor(c, "nd_i", [pad_part, P], I32)
            nd_f = tensor(c, "nd_f", [pad_part, P])
            nd_s = tensor(c, "nd_s", [pad_part, P])
            nd_q = tensor(c, "nd_q", [pad_part, P])
            nd_h = tensor(c, "nd_h", [pad_part, ROWS, P], BF16)
            last_sel = tensor(c, "last_sel", [P, P])
            row_col = tensor(c, "row_col", [P, 1])
            step_col = tensor(c, "step_col", [P, step_cols])
            ends = tensor(c, "ends", [P, n_groups + 1])
            starts = tensor(c, "starts", [P, n_groups + 1])
            span_f = tensor(c, "span_f", [P, n_groups])
            span_i = tensor(c, "span_i", [P, n_groups], I32)
            ones_g = tensor(c, "ones_g", [P, n_groups])
            found = tensor(c, "found", [P, n_groups])
            got = tensor(c, "got", [P, 4, step_cols])
            sb_f = tensor(c, "sb_f", [P, step_cols])
            sg_f = tensor(c, "sg_f", [P, step_cols])
            spare_f = tensor(c, "spare_f", [P, step_cols])
            wide_f = tensor(c, "wide_f", [P, n_table])
            iter_row = tensor(c, "iter_row", [1, most_iter])
            begun = tensor(c, "begun", [1, most_iter])
            iter_f = tensor(c, "iter_f", [1, 1])
            zero_rows = tensor(c, "zero_rows", [P, D])
            wn_nat = tensor(c, "wn_nat", [P, D])
            wa_col = tensor(c, "wa_col", [P, 3])
            we_nat = tensor(c, "we_nat", [P, K64])
            turn = [bank(c, f"turn{i}", 1024) for i in range(2)]
            wide = bank(c, "wide", 1024)
            small = bank(c, "small")
            in_dst, in_src = sem(c, "in_dst"), sem(c, "in_src")
            in_w, in_wdiag, in_x = sem(c, "in_w"), sem(c, "in_wdiag"), sem(c, "in_x")
            p_const, p_ident, v_zero = sem(c, "p_const"), sem(c, "p_ident"), sem(c, "v_zero")
            v_nat, v_chain, t_turned, v_turned = sem(c, "v_nat"), sem(c, "v_chain"), sem(c, "t_turned"), sem(c, "v_turned")
            t_small, t_wide, v_small = sem(c, "t_small"), sem(c, "t_wide"), sem(c, "v_small")
            v_digit, a_square, d_digit, v_sum, d_sum = (sem(c, n) for n in ("v_digit", "a_square", "d_digit", "v_sum", "d_sum"))
            p_node, d_node, d_zero, v_cols = sem(c, "p_node"), sem(c, "d_node"), sem(c, "d_zero"), sem(c, "v_cols")
            block = c.enter_context(nc.Block())
            runs = q_blocks * GROUP

            @block.sync
            def _(sp):
                sp.dma_start(nat_dst[:, :], dst.rearrange("(q e) -> q e", q=q_part)).then_inc(in_dst, 16)
                sp.dma_start(nat_src[:, :], src.rearrange("(q e) -> q e", q=q_part)).then_inc(in_src, 16)
                sp.dma_start(xn[:, 0:x_blocks, :], x.rearrange("(p b) d -> p b d", p=x_part)).then_inc(in_x, 16)
                sp.wait_ge(v_zero, 2)
                for j in range(TILES):
                    sp.dma_start(w_emb_x[j * K16:(j + 1) * K16, j * H:(j + 1) * H], w_emb).then_inc(in_wdiag, 16)
                    sp.dma_start(w_emb_x[TILES * K16:TILES * K16 + 1, j * H:(j + 1) * H],
                                 b_emb.rearrange("(a n) -> a n", a=1)).then_inc(in_wdiag, 16)
                sp.dma_start(h_table.rearrange("(p r) d -> p r d", p=P),
                             zero_rows[:, :].unsqueeze(1).to_broadcast([P, pad_part, D])).then_inc(d_zero, 16)
                for k in range(DIGITS):
                    sp.wait_ge(v_digit, 2 * k + 2)
                    sp.dma_start(pen_edge[1 + k].rearrange("(q e) -> q e", q=q_part), digit_h[:, :]).then_inc(d_digit, 16)
                sp.wait_ge(v_sum, DIGITS)
                sp.dma_start(pen_edge[0].rearrange("(q e) -> q e", q=q_part), sum_h[:, :]).then_inc(d_sum, 16)
                sp.wait_ge(p_node, 1)
                for k in range(ROWS):
                    sp.dma_start(pen_node[k].rearrange("(p r) -> p r", r=P), nd_h[:, k, :]).then_inc(d_node, 16)
                sp.wait_ge(in_wdiag, 16 * 2 * TILES)
                sp.wait_ge(d_zero, 16)
                sp.wait_ge(d_digit, 16 * DIGITS)
                sp.wait_ge(d_sum, 16)
                sp.wait_ge(d_node, 16 * ROWS)
                sp.wait_ge(in_x, 16)

            @block.gpsimd
            def _(pool):
                pool.memset(ident[:, :], 0.0).then_inc(p_ident, 1)
                pool.memset(last_sel[:, :], 0.0).then_inc(p_ident, 1)
                pool.wait_ge(p_ident, 2)
                pool.affine_select(out=ident[:, :], in_=ident[:, :], compare_op=ALU.not_equal, fill=1.0, base=0,
                                   pattern=[[-1, P]], channel_multiplier=1).then_inc(p_const, 1)
                pool.affine_select(out=last_sel[:, :], in_=last_sel[:, :], compare_op=ALU.not_equal, fill=1.0,
                                   base=1 - P, pattern=[[0, P]], channel_multiplier=1).then_inc(p_const, 1)
                pool.iota(row_col[:, :], [[0, 1]], 0, 1, allow_small_or_imprecise_dtypes=True).then_inc(p_const, 1)
                pool.iota(step_col[:, :], [[P, step_cols]], 0, 1, allow_small_or_imprecise_dtypes=True).then_inc(p_const, 1)
                pool.iota(node_i[:, :], [[1, P]], 0, P).then_inc(p_const, 1)
                pool.iota(iter_row[:, :], [[RING, most_iter]], 0, 1, allow_small_or_imprecise_dtypes=True).then_inc(p_const, 1)

            @block.scalar
            def _(act):
                act.dma_start(wn_nat[:, :], wn).then_inc(in_w, 16)
                act.dma_start(we_nat[:, :], we).then_inc(in_w, 16)
                for k in range(3):
                    act.dma_start(wa_col[:, k:k + 1], wa[:, k * D:(k + 1) * D].rearrange("a d -> d a")).then_inc(in_w, 16)
                act.dma_start(w_lin_x[0:H, :], w_lin).then_inc(in_w, 16)
                act.dma_start(w_lin_x[H:H + 1, :], b_lin.rearrange("(a n) -> a n", a=1)).then_inc(in_w, 16)
                for k in range(DIGITS):
                    act.wait_ge(v_digit, 2 * k + 2)
                    if k:
                        act.wait_ge(v_sum, k)
                    act.activation(square_h[:, :], digit_h[:, :], ACT.Square).then_inc(a_square, 1)
                act.wait_ge(in_w, 112)

            @block.tensor
            def _(pe):
                pe.wait_ge(p_const, 2)
                pe.wait_ge(in_w, 112)
                pe.transpose(small[:, 0:D], wn_nat[:, :], ident[:, :])
                pe.matmul(small[:, D:D + 2], wn_nat[:, :], wa_col[:, 0:2], start=True, stop=True)
                pe.matmul(small[:, 256:256 + K64], wa_col[:, 2:3].to_broadcast([P, P]), we_nat[:, :],
                          start=True, stop=True).then_inc(t_small, 1)
                n = 0
                for t in range(2):
                    for b in range(q_blocks):
                        if b == 0:
                            pe.wait_ge(v_nat, t + 1)
                        if n >= 2:
                            pe.wait_ge(v_turned, n - 1)
                        for j in range(TILES):
                            at = j * q_part if j < 4 else 512
                            ins = pe.transpose(turn[n % 2][:, at:at + q_part],
                                               nat_f[:, b * GROUP + j:(b + 1) * GROUP:TILES],
                                               ident[0:q_part, 0:q_part])
                        ins.then_inc(t_turned, 1)
                        n += 1
                pe.wait_ge(v_turned, q_blocks)
                ends_in = dst_e[:, :, :, TILES - 1].rearrange("p q b -> p (q b)")
                for lo in range(0, n_groups, 512):
                    hi = min(lo + 512, n_groups)
                    ins = pe.matmul(wide[:, lo:hi], last_sel[:, :], ends_in[:, lo:hi], start=True, stop=True)
                ins.then_inc(t_wide, 1)
                pe.wait_ge(v_cols, 1)
                for k in range(step_cols):
                    ins = pe.matmul(wide[:, k * P:(k + 1) * P], sb_f[:, k:k + 1].to_broadcast([P, P]), ident[:, :],
                                    start=True, stop=True)
                ins.then_inc(t_wide, 1)
                for k in range(step_cols):
                    ins = pe.matmul(turn[0][:, k * P:(k + 1) * P], sg_f[:, k:k + 1].to_broadcast([P, P]), ident[:, :],
                                    start=True, stop=True)
                ins.then_inc(t_wide, 1)

            @block.vector
            def _(v):
                chain = [0]

                def then(ins):
                    chain[0] += 1
                    ins.then_inc(v_chain, 1)
                    v.wait_ge(v_chain, chain[0])

                v.memset(w_emb_x[:, :], 0.0).then_inc(v_zero, 1)
                v.memset(zero_rows[:, :], 0.0).then_inc(v_zero, 1)
                v.memset(ones_g[:, :], 1.0)
                v.memset(eps[:, :], LN_EPS)
                v.memset(ends[:, 0:1], 0.0)
                then(v.memset(starts[:, 0:1], 0.0))
                n = 0
                for t, (nat, arrived) in enumerate(((nat_dst, in_dst), (nat_src, in_src))):
                    v.wait_ge(arrived, 16)
                    if t:
                        v.wait_ge(t_turned, q_blocks)
                    v.tensor_copy(nat_f[:, :], nat[:, :]).then_inc(v_nat, 1)
                    for b in range(q_blocks):
                        v.wait_ge(t_turned, n + 1)
                        to = (dst_e, src_e)[t]
                        v.tensor_copy(to[:, :, b, 0:4].rearrange("p q j -> p j q"),
                                      turn[n % 2][:, 0:4 * q_part].rearrange("p (j q) -> p j q", j=4))
                        v.tensor_copy(to[:, :, b, 4], turn[n % 2][:, 512:512 + q_part]).then_inc(v_turned, 1)
                        n += 1
                v.wait_ge(t_small, 1)
                v.tensor_copy(wn_x[:, :], small[:, 0:D + 2])
                v.tensor_copy(v_edge[:, :], small[:, 256:256 + K64])
                v.wait_ge(t_wide, 1)
                then(v.tensor_copy(ends[:, 1:n_groups + 1], wide[:, 0:n_groups]))
                then(v.tensor_tensor(span_i[:, :], ends[:, 1:n_groups + 1], ends[:, 0:n_groups], ALU.subtract))
                then(v.tensor_scalar(span_i[:, :], span_i[:, :], 6, None, ALU.arith_shift_right))
                then(v.tensor_copy(span_f[:, :], span_i[:, :]))
                then(v.tensor_tensor_scan(starts[:, 1:n_groups + 1], span_f[:, :], ones_g[:, :], 0.0, ALU.add, ALU.add))
                v.wait_ge(p_const, 6)
                then(v.tensor_scalar(begun[:, :], iter_row[:, :], starts[0:1, n_groups:n_groups + 1], None, ALU.is_lt))
                then(v.tensor_reduce(iter_f[:, :], begun[:, :], AX.X, ALU.add))
                then(v.tensor_copy(n_iter[:, :], iter_f[:, :]))
                for k in range(step_cols):
                    s = step_col[:, k:k + 1]
                    then(v.tensor_scalar(found[:, :], starts[:, 0:n_groups], s, None, ALU.is_le))
                    then(v.tensor_reduce(got[:, 0, k:k + 1], found[:, :], AX.X, ALU.add))
                    then(v.scalar_tensor_tensor(out=found[:, :], in0=starts[:, 0:n_groups], scalar=s,
                                                in1=starts[:, 0:n_groups], op0=ALU.is_le, op1=ALU.mult))
                    then(v.tensor_reduce(got[:, 1, k:k + 1], found[:, :], AX.X, ALU.max))
                    then(v.scalar_tensor_tensor(out=found[:, :], in0=starts[:, 0:n_groups], scalar=s,
                                                in1=ends[:, 0:n_groups], op0=ALU.is_le, op1=ALU.mult))
                    then(v.tensor_reduce(got[:, 2, k:k + 1], found[:, :], AX.X, ALU.max))
                then(v.tensor_scalar(sg_f[:, :], got[:, 0, :], 1.0, None, ALU.subtract))
                then(v.tensor_tensor(got[:, 3, :], step_col[:, :], got[:, 1, :], ALU.subtract))
                then(v.scalar_tensor_tensor(out=sb_f[:, :], in0=got[:, 3, :], scalar=float(W), in1=got[:, 2, :],
                                            op0=ALU.mult, op1=ALU.add))
                then(v.tensor_scalar(spare_f[:, :], step_col[:, :], starts[:, n_groups:n_groups + 1], None, ALU.is_ge))
                then(v.tensor_scalar(got[:, 3, :], sb_f[:, :], -1.0, float(spare), ALU.mult, ALU.add))
                then(v.tensor_tensor(got[:, 3, :], got[:, 3, :], spare_f[:, :], ALU.mult))
                v.tensor_tensor(sb_f[:, :], sb_f[:, :], got[:, 3, :], ALU.add).then_inc(v_cols, 1)
                for k in range(DIGITS):
                    if k:
                        v.wait_ge(d_digit, 16 * k)
                        v.wait_ge(a_square, k)
                    v.tensor_scalar(digit_i[:, :], nat_dst[:, :], 3 * k, 7, ALU.arith_shift_right,
                                    ALU.bitwise_and).then_inc(v_digit, 1)
                    v.wait_ge(v_digit, 2 * k + 1)
                    v.tensor_copy(digit_h[:, :], digit_i[:, :]).then_inc(v_digit, 1)
                    v.wait_ge(a_square, k + 1)
                    if k == 0:
                        v.tensor_copy(sum_h[:, :], square_h[:, :]).then_inc(v_sum, 1)
                    else:
                        v.wait_ge(v_sum, k)
                        v.tensor_tensor(sum_h[:, :], sum_h[:, :], square_h[:, :], ALU.add).then_inc(v_sum, 1)
                for k in range(DIGITS):
                    then(v.tensor_scalar(nd_i[:, :], node_i[:, :], 3 * k, 7, ALU.arith_shift_right, ALU.bitwise_and))
                    then(v.tensor_copy(nd_f[:, :], nd_i[:, :]))
                    then(v.tensor_scalar(nd_h[:, 2 + k, :], nd_f[:, :], 2.0 * PENALTY, None, ALU.mult))
                    if k == 0:
                        then(v.tensor_tensor(nd_s[:, :], nd_f[:, :], nd_f[:, :], ALU.mult))
                    else:
                        then(v.tensor_tensor(nd_q[:, :], nd_f[:, :], nd_f[:, :], ALU.mult))
                        then(v.tensor_tensor(nd_s[:, :], nd_s[:, :], nd_q[:, :], ALU.add))
                then(v.memset(nd_h[:, 1, :], -PENALTY))
                v.tensor_scalar(nd_h[:, 0, :], nd_s[:, :], -PENALTY, None, ALU.mult).then_inc(p_node, 1)
                v.wait_ge(t_wide, 2)
                then(v.tensor_copy(base_f[:, :], wide[:, 0:n_table]))
                then(v.tensor_tensor(wide_f[:, 1:n_table], base_f[:, 1:n_table], base_f[:, 0:n_table - 1], ALU.subtract))
                then(v.memset(wide_f[:, 0:1], -1.0))
                then(v.tensor_scalar(carry_sel[:, :], wide_f[:, :], row_col[:, 0:1], None, ALU.is_equal))
                v.wait_ge(t_wide, 3)
                v.scalar_tensor_tensor(out=step_gb[:, :], in0=turn[0][0:1, 0:n_table], scalar=float(2 ** NODE_BITS),
                                       in1=base_f[0:1, :], op0=ALU.mult, op1=ALU.add).then_inc(tables_done, 1)
                v.wait_ge(tables_done, 1)

        KT = TILES * K16
        last_g = n_groups - 1

        def iterations(eng):
            return eng.value_load(n_iter[0:1, 0:1], min_val=-(-n_groups // RING), max_val=most_iter)

        def alone(eng):
            eng.sem_inc(waits_passed, 1)

        def steps_from(engine, s, count):
            loaded = nc.values_load_multi_w_load_instructions(
                step_gb[0:1, bass.ds(s, count)], engines=[engine], min_val=0, max_val=last_g * 2 ** NODE_BITS + spare)
            return loaded[1]

        def group_of(eng, entry):
            return nc.s_assert_within(eng.snap(entry >> NODE_BITS), 0, last_g,
                                      skip_runtime_bounds_check_because="the table holds groups")

        def base_of(eng, entry):
            return nc.s_assert_within(eng.snap(entry & (2 ** NODE_BITS - 1)), 0, spare,
                                      skip_runtime_bounds_check_because="the table holds windows")

        with ExitStack() as layer0:
            acc = tensor(layer0, "acc", [H + 1, n_pad])
            with ExitStack() as c:
                lnx = tensor(c, "lnx", [x_part, x_blocks, 6])
                mv = tensor(c, "mv", [x_part, x_blocks, 2])
                rstd = tensor(c, "rstd", [x_part, x_blocks])
                shift = tensor(c, "shift", [x_part, x_blocks])
                spread = tensor(c, "spread", [x_part, x_blocks])
                ln_sqrt = sem(c, "ln_sqrt")
                h0 = tensor(c, "h0", [x_part, 4, D])
                ea = tensor(c, "ea", [P, RING, KT + 1])
                offs = tensor(c, "offs", [P, RING, TILES])
                cols = tensor(c, "cols", [P, TILES, W])
                hot = tensor(c, "hot", [P, 2, TILES, W])
                ea_t = tensor(c, "ea_t", [KT + 1, 2, P])
                hid = tensor(c, "hid", [P, 2, TILES, H + 1])
                ps_t = [bank(c, f"ps_t{i}") for i in range(2)]
                ps_u = [bank(c, f"ps_u{i}") for i in range(2)]
                ps_s = [bank(c, f"ps_s{i}") for i in range(2)]
                ea_in = [sem(c, f"ea_in{u}") for u in range(RING)]
                const0, zeroed = sem(c, "const0"), sem(c, "zeroed")
                turned, copied, embedded, activated, summed, added = (
                    sem(c, n) for n in ("turned", "copied", "embedded", "activated", "summed", "added"))
                offset_set, hot_set = sem(c, "offset_set"), sem(c, "hot_set")
                ln_stat, ln_chain, ln_scale, ln_act, ln_add = (
                    sem(c, n) for n in ("ln_stat", "ln_chain", "ln_scale", "ln_act", "ln_add"))
                block = c.enter_context(nc.Block())
                ea_v = ea16.rearrange("(g p j) k -> g p (j k)", p=P, j=TILES)

                @block.sync
                def _(sp):
                    sp.wait_ge(const0, 3)
                    n = iterations(sp)

                    def load(entry, u):
                        g = group_of(sp, entry)
                        sp.dma_start(ea[:, u, 0:KT], ea_v[bass.ds(g, 1)].rearrange("a p k -> (a p) k")).then_inc(ea_in[u], 16)

                    first = steps_from(mybir.EngineType.SP, 0, RING)
                    for u in range(RING):
                        load(first[u], u)
                    with sp.Fori(0, n) as i:
                        ahead = steps_from(mybir.EngineType.SP, i * RING + RING, RING)
                        for u in range(RING):
                            sp.wait_ge(turned, i * RING + (u + 1))
                            alone(sp)
                            load(ahead[u], u)
                    for u in range(RING):
                        sp.wait_ge(ea_in[u], n * 16 + 16)
                        alone(sp)

                @block.gpsimd
                def _(pool):
                    pool.iota(cols[:, :, :], [[0, TILES], [1, W]], 0, 0, allow_small_or_imprecise_dtypes=True).then_inc(const0, 1)
                    n = iterations(pool)

                    def offset(entry, s, u):
                        g = group_of(pool, entry)
                        pool.tensor_tensor(offs[:, u, :], flat_dst[:, bass.ds(g * TILES, TILES)],
                                           base_f[:, bass.ds(s, 1)].to_broadcast([P, TILES]), ALU.subtract).then_inc(offset_set, 1)

                    first = steps_from(mybir.EngineType.Pool, 0, RING)
                    for u in range(RING):
                        offset(first[u], u, u)
                    with pool.Fori(0, n) as i:
                        ahead = steps_from(mybir.EngineType.Pool, i * RING + RING, RING)
                        for u in range(RING):
                            pool.wait_ge(hot_set, i * RING + (u + 1))
                            offset(ahead[u], i * RING + (u + RING), u)
                    for b in range(x_blocks):
                        pool.wait_ge(ln_act, b + 1)
                        pool.tensor_tensor(xn[:, b, :], xn[:, b, :], h0[:, b % 4, :], ALU.add).then_inc(ln_add, 1)

                @block.scalar
                def _(act):
                    n = iterations(act)

                    def copy_t(s, u):
                        act.wait_ge(turned, s + 1)
                        act.activation(ea_t[:, u % 2, :], ps_t[u % 2][0:KT + 1, 0:P], ACT.Copy).then_inc(copied, 1)

                    def silu(s, u):
                        act.wait_ge(embedded, s + 1)
                        act.activation(hid[:, u % 2, :, 0:H], ps_u[u % 2][:, 0:TILES * H].rearrange("p (j h) -> p j h", j=TILES),
                                       ACT.Silu).then_inc(activated, 1)

                    act.wait_ge(ln_chain, x_blocks)
                    act.activation(spread[:, :], mv[:, :, 1], ACT.Sqrt, bias=eps[:, :]).then_inc(ln_sqrt, 1)
                    act.wait_ge(const0, 3)
                    copy_t(0, 0)
                    copy_t(1, 1)
                    silu(0, 0)
                    with act.Fori(0, n) as i:
                        for u in range(RING):
                            s = i * RING + u
                            act.wait_ge(embedded, s + 1)
                            copy_t(s + 2, u)
                            act.wait_ge(summed, s + 1)
                            silu(s + 1, u + 1)
                    act.wait_ge(ln_scale, 1)
                    for b in range(x_blocks):
                        if b >= 4:
                            act.wait_ge(ln_add, b - 3)
                        act.activation(h0[:, b % 4, :], xn[:, b, :], ACT.Relu, bias=shift[:, b:b + 1],
                                       scale=rstd[:, b:b + 1]).then_inc(ln_act, 1)

                @block.tensor
                def _(pe):
                    n = iterations(pe)
                    pe.sem_inc(summed, 1)

                    def turn_edges(s, u):
                        pe.transpose(ps_t[u % 2][0:KT + 1, 0:P], ea[:, u % RING, :], ident[:, :]).then_inc(turned, 1)

                    def embed(s, u):
                        pe.wait_ge(copied, s + 1)
                        pe.matmul(ps_u[u % 2][:, 0:TILES * H], ea_t[:, u % 2, :], w_emb_x[:, :], start=True,
                                  stop=True).then_inc(embedded, 1)

                    def sum_up(s, u):
                        pe.wait_ge(activated, s + 1)
                        pe.wait_ge(hot_set, s + 1)
                        pe.wait_ge(added, s + 1)
                        for j in range(TILES):
                            ins = pe.matmul(ps_s[u % 2][0:H + 1, 0:W], hid[:, u % 2, j, :], hot[:, u % 2, j, :],
                                            start=(j == 0), stop=(j == TILES - 1))
                        ins.then_inc(summed, 1)

                    pe.wait_ge(const0, 3)
                    pe.wait_ge(ea_in[0], 16)
                    turn_edges(0, 0)
                    pe.wait_ge(ea_in[1], 16)
                    turn_edges(1, 1)
                    embed(0, 0)
                    with pe.Fori(0, n) as i:
                        for u in range(RING):
                            s = i * RING + u
                            pe.wait_ge(ea_in[(u + 2) % RING], i * 16 + 16 * (1 + (u + 2) // RING))
                            pe.wait_ge(copied, s + 1)
                            turn_edges(s + 2, u + 2)
                            embed(s + 1, u + 1)
                            sum_up(s, u)

                @block.vector
                def _(v):
                    v.sem_inc(added, 2)
                    v.memset(ea[:, :, KT:KT + 1], 1.0).then_inc(const0, 1)
                    v.memset(hid[:, :, :, H:H + 1], 1.0).then_inc(const0, 1)
                    v.memset(xn[:, x_blocks:x_blocks + 4, :], 0.0)
                    v.memset(acc[:, :], 0.0).then_inc(zeroed, 1)
                    for b in range(x_blocks):
                        v.bn_stats(lnx[:, b, :], xn[:, b, :]).then_inc(ln_stat, 1)
                    for b in range(x_blocks):
                        v.wait_ge(ln_stat, b + 1)
                        v.bn_aggr(mv[:, b, :], lnx[:, b, :]).then_inc(ln_chain, 1)
                    v.wait_ge(ln_chain, x_blocks)
                    v.wait_ge(ln_sqrt, 1)
                    v.reciprocal(rstd[:, :], spread[:, :]).then_inc(ln_chain, 1)
                    v.wait_ge(ln_chain, x_blocks + 1)
                    v.scalar_tensor_tensor(out=shift[:, :], in0=mv[:, :, 0], scalar=-1.0, in1=rstd[:, :],
                                           op0=ALU.mult, op1=ALU.mult).then_inc(ln_scale, 1)
                    v.wait_ge(zeroed, 1)
                    v.wait_ge(const0, 3)
                    n = iterations(v)

                    def one_hot(s, u):
                        v.wait_ge(offset_set, s + 1)
                        v.tensor_tensor(hot[:, u % 2], cols[:, :, :],
                                        offs[:, u % RING, :].unsqueeze(2).to_broadcast([P, TILES, W]),
                                        ALU.is_equal).then_inc(hot_set, 1)

                    one_hot(0, 0)
                    with v.Fori(0, n) as i:
                        steps = steps_from(mybir.EngineType.DVE, i * RING, RING)
                        for u in range(RING):
                            s = i * RING + u
                            v.wait_ge(summed, s + 1)
                            one_hot(s + 1, u + 1)
                            b = base_of(v, steps[u])
                            v.wait_ge(summed, s + 2)
                            v.wait_ge(added, s + 2)
                            v.tensor_tensor(acc[:, bass.ds(b, W)], acc[:, bass.ds(b, W)], ps_s[u % 2][0:H + 1, 0:W],
                                            ALU.add).then_inc(added, 1)

            with ExitStack() as c:
                CH = 2
                chunks = x_blocks // CH
                assert chunks % 2 == 0
                stats = tensor(c, "stats", [x_part, 2, CH, 6])
                mv = tensor(c, "mv1", [x_part, 2, CH, 2])
                rstd = tensor(c, "rstd1", [x_part, 2, CH])
                shift = tensor(c, "shift1", [x_part, 2, CH])
                spread = tensor(c, "spread1", [x_part, 2, CH])
                spread_set = sem(c, "spread_set")
                acc_n = tensor(c, "acc_n", [H + 1, 2, CH, x_part])
                h1 = tensor(c, "h1", [x_part, 2, CH, D])
                h1_t = tensor(c, "h1_t", [D, 2, CH * x_part])
                z_out = tensor(c, "z_out", [x_part, 2, CH, Z])
                q_out = tensor(c, "q_out", [x_part, x_blocks])
                q_zero = tensor(c, "q_zero", [1, n_pad - n_nodes])
                ps_x = [bank(c, f"ps_x{i}") for i in range(2)]
                ps_h = [bank(c, f"ps_h{i}") for i in range(2)]
                ps_z = [bank(c, f"ps_z{i}") for i in range(2)]
                acc_copied, x1_sum, x1_set, stat_set, mv_set, rstd_set, shift_set = (
                    sem(c, n) for n in ("acc_copied", "x1_sum", "x1_set", "stat_set", "mv_set", "rstd_set", "shift_set"))
                h1_set, h1_turned, h1_copied, z_sum, z_set, q_set = (
                    sem(c, n) for n in ("h1_set", "h1_turned", "h1_copied", "z_sum", "z_set", "q_set"))
                z_stored = [sem(c, f"z_stored{u}") for u in range(2)]
                z_free, q_stored, q_zeroed = sem(c, "z_free"), sem(c, "q_stored"), sem(c, "q_zeroed")
                block = c.enter_context(nc.Block())

                @block.sync
                def _(sp):
                    z_v = z_table.rearrange("(p b) c -> p b c", p=x_part)
                    with sp.Fori(0, chunks // 2) as i:
                        for u in range(2):
                            sp.wait_ge(z_set, i * 2 + (u + 1))
                            sp.dma_start(z_v[:, bass.ds(i * (2 * CH) + u * CH, CH), :], z_out[:, u, :, :]).then_inc(z_stored[u], 16)
                            sp.wait_ge(z_stored[u], i * 16 + 16)
                            sp.sem_inc(z_free, 1)
                    sp.wait_ge(q_set, chunks)
                    sp.wait_ge(q_zeroed, 1)
                    sp.dma_start(q_table[0:n_nodes].rearrange("(p b) c -> p (b c)", p=x_part), q_out[:, :]).then_inc(q_stored, 16)
                    sp.dma_start(q_table[n_nodes:n_pad].rearrange("n a -> a n"), q_zero[:, :]).then_inc(q_stored, 16)
                    sp.wait_ge(q_stored, 32)

                @block.scalar
                def _(act):
                    def copy_acc(b, u):
                        for k in range(CH):
                            ins = act.activation(acc_n[:, u % 2, k, :].unsqueeze(2),
                                                 acc[:, bass.ds(b + k, (x_part - 1) * x_blocks + 1)][:, 0:(x_part - 1) * x_blocks + 1:x_blocks].unsqueeze(2),
                                                 ACT.Copy)
                        ins.then_inc(acc_copied, 1)

                    def root(c0, u):
                        act.wait_ge(mv_set, c0 + 1)
                        act.activation(spread[:, u % 2, :], mv[:, u % 2, :, 1], ACT.Sqrt,
                                       bias=eps[:, :]).then_inc(spread_set, 1)

                    copy_acc(0, 0)
                    copy_acc(CH, 1)
                    root(0, 0)
                    with act.Fori(0, chunks // 2) as i:
                        for u in range(2):
                            c0 = i * 2 + u
                            act.wait_ge(shift_set, c0 + 1)
                            for k in range(CH):
                                b = c0 * CH + k
                                ins = act.activation(h1[:, u, k, :], xn[:, bass.ds(b, 1), :].rearrange("p a d -> p (a d)"), ACT.Relu,
                                                     bias=shift[:, u, k:k + 1], scale=rstd[:, u, k:k + 1])
                            ins.then_inc(h1_set, 1)
                            act.wait_ge(x1_sum, c0 + 1)
                            copy_acc(c0 * CH + 2 * CH, u)
                            root(c0 + 1, u + 1)
                            act.wait_ge(h1_turned, c0 + 1)
                            act.wait_ge(z_sum, c0 + 1)
                            act.activation(h1_t[:, u, :], ps_h[u][:, 0:CH * x_part], ACT.Copy).then_inc(h1_copied, 1)

                @block.tensor
                def _(pe):
                    pe.sem_inc(z_sum, 2)

                    def x_sum(c0, u):
                        pe.wait_ge(acc_copied, c0 + 1)
                        for k in range(CH):
                            ins = pe.matmul(ps_x[u % 2][0:x_part, k * D:(k + 1) * D], acc_n[:, u % 2, k, :], w_lin_x[:, :],
                                            start=True, stop=True)
                        ins.then_inc(x1_sum, 1)

                    x_sum(0, 0)
                    with pe.Fori(0, chunks // 2) as i:
                        for u in range(2):
                            c0 = i * 2 + u
                            pe.wait_ge(h1_set, c0 + 1)
                            for k in range(CH):
                                ins = pe.transpose(ps_h[u][:, k * x_part:(k + 1) * x_part], h1[:, u, k, :],
                                                   ident[0:x_part, 0:x_part])
                            ins.then_inc(h1_turned, 1)
                            x_sum(c0 + 1, u + 1)
                            pe.wait_ge(h1_copied, c0 + 1)
                            for k in range(CH):
                                ins = pe.matmul(ps_z[u][0:x_part, k * (D + 2):(k + 1) * (D + 2)],
                                                h1_t[:, u, k * x_part:(k + 1) * x_part], wn_x[:, :], start=True, stop=True)
                            ins.then_inc(z_sum, 1)

                @block.vector
                def _(v):
                    v.memset(q_zero[:, :], 0.0).then_inc(q_zeroed, 1)
                    v.sem_inc(z_free, 2)

                    def x_one(c0, u):
                        b = c0 * CH
                        v.wait_ge(x1_sum, c0 + 1)
                        xs = xn[:, bass.ds(b, CH), :]
                        v.tensor_tensor(xs, xs, ps_x[u % 2][0:x_part, 0:CH * D].rearrange("p (k d) -> p k d", k=CH),
                                        ALU.add).then_inc(x1_set, 1)
                        v.wait_ge(x1_set, c0 + 1)
                        alone(v)
                        for k in range(CH):
                            ins = v.bn_stats(stats[:, u % 2, k, :],
                                             xn[:, bass.ds(b + k, 1), :].rearrange("p a d -> p (a d)"))
                        ins.then_inc(stat_set, 1)
                        v.wait_ge(stat_set, c0 + 1)
                        alone(v)
                        for k in range(CH):
                            ins = v.bn_aggr(mv[:, u % 2, k, :], stats[:, u % 2, k, :])
                        ins.then_inc(mv_set, 1)
                        v.wait_ge(spread_set, c0 + 1)
                        v.reciprocal(rstd[:, u % 2, :], spread[:, u % 2, :]).then_inc(rstd_set, 1)
                        v.wait_ge(rstd_set, c0 + 1)
                        v.scalar_tensor_tensor(out=shift[:, u % 2, :], in0=mv[:, u % 2, :, 0], scalar=-1.0,
                                               in1=rstd[:, u % 2, :], op0=ALU.mult, op1=ALU.mult).then_inc(shift_set, 1)

                    x_one(0, 0)
                    with v.Fori(0, chunks // 2) as i:
                        for u in range(2):
                            c0 = i * 2 + u
                            x_one(c0 + 1, u + 1)
                            v.wait_ge(z_free, c0 + 1)
                            v.wait_ge(z_sum, c0 + 3)
                            z = ps_z[u][0:x_part, 0:CH * (D + 2)].rearrange("p (k d) -> p k d", k=CH)
                            v.tensor_copy(z_out[:, u, :, :], z[:, :, 0:Z]).then_inc(z_set, 1)
                            v.tensor_copy(q_out[:, bass.ds(c0 * CH, CH)], z[:, :, D + 1]).then_inc(q_set, 1)

        with ExitStack() as c:
            edge_f = tensor(c, "edge_f", [P, RING, TILES, K64])
            index = tensor(c, "index", [P, RING, TILES], I32)
            rows = tensor(c, "rows", [P, RING, TILES, ZC])
            pen_e = tensor(c, "pen_e", [ROWS, RING, GROUP], BF16)
            pen_n = tensor(c, "pen_n", [ROWS, RING, W], BF16)
            q_win = tensor(c, "q_win", [W, RING])
            sel = tensor(c, "sel", [W, RING])
            product = tensor(c, "product", [P, TILES, K64])
            edge_r = tensor(c, "edge_r", [P, TILES])
            logit = tensor(c, "logit", [P, 2, TILES])
            top = tensor(c, "top", [W, 1])
            top_q = tensor(c, "top_q", [W, 1])
            top_l = tensor(c, "top_l", [W, 1])
            peak = tensor(c, "peak", [W, 2])
            carried = tensor(c, "carried", [W, 1])
            bias1 = tensor(c, "bias1", [W, 1])
            bias2 = tensor(c, "bias2", [W, 1])
            valid = tensor(c, "valid", [1, 1])
            fade = tensor(c, "fade", [1, 2])
            prob1 = tensor(c, "prob1", [W, GROUP])
            prob2 = tensor(c, "prob2", [W, GROUP])
            prob_t = tensor(c, "prob_t", [P, TILES, W])
            prob_a = tensor(c, "prob_a", [P, TILES * W])
            row0 = tensor(c, "row0", [1, W])
            carry_in = tensor(c, "carry_in", [1, ZC])
            total = tensor(c, "total", [W, ZC])
            weight = tensor(c, "weight", [W, 1])
            inverse = tensor(c, "inverse", [W, 1])
            h_out = tensor(c, "h_out", [W, RING, D])
            ps_m = [bank(c, f"ps_m{i}", 1024, W) for i in range(2)]
            ps_p1 = bank(c, "ps_p1")
            ps_p2 = bank(c, "ps_p2")
            ps_o = bank(c, "ps_o")
            ps_cm = ps_o[:, 256:258]
            ps_ca = bank(c, "ps_ca")
            const1 = sem(c, "const1")
            index_in = [sem(c, f"index_in{u}") for u in range(RING)]
            sel_in = [sem(c, f"sel_in{half}") for half in range(2)]
            loads_in = [sem(c, f"loads_in{u}") for u in range(RING)]
            rows_in = [sem(c, f"rows_in{u}") for u in range(RING)]
            product_set, r_set, logit_set, scored, top_set, topq_set, topl_set, peak_set, bias1_set, bias2_set = (
                sem(c, n) for n in ("product_set", "r_set", "logit_set", "scored", "top_set", "topq_set", "topl_set",
                                    "peak_set", "bias1_set", "bias2_set"))
            peak_carried, valid_set, carried_set, fade_set, prob_set, prob_turned, prob_t_set = (
                sem(c, n) for n in ("peak_carried", "valid_set", "carried_set", "fade_set", "prob_set", "prob_turned",
                                    "prob_t_set"))
            total_carried, carry_set, summed, total_set, weight_set, inverse_set, h_set, h_free = (
                sem(c, n) for n in ("total_carried", "carry_set", "summed1", "total_set", "weight_set", "inverse_set",
                                    "h_set", "h_free"))
            prob_copied = sem(c, "prob_copied")
            h_stored = [sem(c, f"h_stored{u}") for u in range(2)]
            CONSTS = 5
            block = c.enter_context(nc.Block())
            ea_v = ea64.rearrange("(g p j) k -> g p (j k)", p=P, j=TILES)

            @block.sync
            def _(sp):
                sp.wait_ge(const1, CONSTS)
                n = iterations(sp)

                def load_index(entry, u):
                    g = group_of(sp, entry)
                    sp.dma_start(index[:, u, :], flat_src[:, bass.ds(g * TILES, TILES)]).then_inc(index_in[u], 16)

                def load(entry, u):
                    g = group_of(sp, entry)
                    b = base_of(sp, entry)
                    for to, of in ((edge_f[:, u, :, :].rearrange("p j k -> p (j k)"), ea_v[bass.ds(g, 1)].rearrange("a p k -> (a p) k")),
                                   (pen_e[1:ROWS, u, :], pen_edge[:, bass.ds(g * GROUP, GROUP)]),
                                   (pen_n[:, u, :], pen_node[:, bass.ds(b, W)]),
                                   (q_win[:, u:u + 1], q_table[bass.ds(b, W), :])):
                        sp.dma_start(to, of).then_inc(loads_in[u], 16)

                def load_sel(s, half):
                    sp.dma_start(sel[:, half * HALF:(half + 1) * HALF], carry_sel[0:W, bass.ds(s, HALF)]).then_inc(sel_in[half], 16)

                first = steps_from(mybir.EngineType.SP, 0, RING)
                for u in range(RING):
                    load_index(first[u], u)
                for u in range(RING):
                    if u % HALF == 0:
                        load_sel(u, u // HALF)
                    load(first[u], u)
                sp.wait_ge(h_set, 1)
                sp.dma_start(h_table[spare:spare + W, :], h_out[:, RING - 1, :]).then_inc(h_stored[1], 16)
                with sp.Fori(0, n) as i:
                    steps = steps_from(mybir.EngineType.SP, i * RING, 2 * RING)
                    for u in range(RING):
                        s = i * RING + u
                        sp.wait_ge(rows_in[u], i * 80 + 80)
                        load_index(steps[u + RING], u)
                        sp.wait_ge(total_carried, s + 1)
                        alone(sp)
                        if u % HALF == HALF - 1:
                            load_sel(s + (RING + 1 - HALF), u // HALF)
                        load(steps[u + RING], u)
                        b = base_of(sp, steps[u])
                        sp.wait_ge(h_set, s + 2)
                        alone(sp)
                        sp.wait_ge(h_stored[(u + 1) % 2], i * (RING // 2 * 16) + 16 * (1 + u // 2))
                        sp.sem_inc(h_free, 1)
                        sp.dma_start(h_table[bass.ds(b, W), :], h_out[:, u, :]).then_inc(h_stored[u % 2], 16)
                for u in range(RING):
                    sp.wait_ge(index_in[u], n * 16 + 16)
                    sp.wait_ge(loads_in[u], n * 64 + 64)
                for half in range(2):
                    sp.wait_ge(sel_in[half], n * 16 + 16)
                sp.wait_ge(h_stored[1], n * (RING // 2 * 16) + 16)
                sp.wait_ge(h_stored[0], n * (RING // 2 * 16))
                alone(sp)

            @block.gpsimd
            def _(pool):
                n = iterations(pool)

                def gather(u, count):
                    pool.wait_ge(index_in[u], count)
                    alone(pool)
                    for j in range(TILES):
                        pool.indirect_dma_start(rows[:, u, j, 0:Z], None, z_table,
                                                bass.IndirectOffsetOnAxis(ap=index[:, u, j:j + 1], axis=0)).then_inc(rows_in[u], 16)

                pool.wait_ge(const1, CONSTS)
                pool.sem_inc(summed, 1)
                for u in range(RING - 1):
                    gather(u, 16)
                with pool.Fori(0, n) as i:
                    for u in range(RING):
                        pool.wait_ge(summed, i * RING + u + 1)
                        alone(pool)
                        gather((u + RING - 1) % RING, i * 16 + 16 * (1 + (u + RING - 1) // RING))
                for u in range(RING - 1):
                    pool.wait_ge(rows_in[u], n * 80 + 80)
                    alone(pool)

            @block.scalar
            def _(act):
                n = iterations(act)

                def exps(s, u):
                    act.wait_ge(bias2_set, s + 1)
                    act.activation(fade[:, u % 2:u % 2 + 1], peak[0:1, 0:1], ACT.Exp, bias=carried[0:1, :], scale=-1.0).then_inc(fade_set, 1)
                    act.activation(prob1[:, :], ps_m[u % 2][:, 0:GROUP], ACT.Exp, bias=bias1[:, :])
                    act.activation(prob2[:, :], ps_m[u % 2][:, 0:GROUP], ACT.Exp, bias=bias2[:, :], scale=0.2).then_inc(prob_set, 1)

                def set_h(s, u):
                    act.wait_ge(inverse_set, s + 1)
                    act.wait_ge(h_free, s + 1)
                    act.activation(h_out[:, u % RING, :], total[:, 0:D], ACT.Copy, scale=inverse[:, 0:1]).then_inc(h_set, 1)

                act.wait_ge(const1, CONSTS)
                exps(0, 0)
                with act.Fori(0, n) as i:
                    for u in range(RING):
                        s = i * RING + u
                        set_h(s, u + RING - 1)
                        act.wait_ge(prob_turned, s * 2 + 1)
                        act.activation(prob_a[:, :], ps_p1[:, 0:TILES * W], ACT.Copy).then_inc(prob_copied, 1)
                        act.wait_ge(total_carried, s + 1)
                        act.wait_ge(fade_set, s + 1)
                        act.activation(carry_in[:, :], ps_ca[0:1, 0:ZC], ACT.Copy, scale=fade[0:1, u % 2:u % 2 + 1]).then_inc(carry_set, 1)
                        exps(s + 1, u + 1)
                set_h(n * RING, RING - 1)

            @block.tensor
            def _(pe):
                n = iterations(pe)

                def score(s, u, count):
                    pe.wait_ge(loads_in[u], count)
                    pe.wait_ge(logit_set, s + 1)
                    for lo, hi in ((0, 4), (4, 5)):
                        e = pen_e[:, u, :].rearrange("r (p j) -> r j p", j=TILES)[:, lo:hi, :]
                        pe.matmul(ps_m[u % 2][:, lo * P:hi * P], pen_n[:, u, :], e, start=True, stop=False)
                    for j in range(TILES):
                        ins = pe.matmul(ps_m[u % 2][:, j * P:(j + 1) * P], logit[:, u % 2, j:j + 1].to_broadcast([P, W]), ident[:, :],
                                        start=False, stop=(j >= 3))
                    ins.then_inc(scored, 1)

                def carry_peak(s, u, i):
                    pe.wait_ge(peak_set, s)
                    alone(pe)
                    pe.wait_ge(total_set, s)
                    alone(pe)
                    if u % HALF == 0:
                        pe.wait_ge(sel_in[u // HALF], i * 16 + 16 * (1 if u else 2))
                        alone(pe)
                    pe.matmul(ps_cm[0:1, :], sel[:, u:u + 1], peak[:, :], start=True, stop=True).then_inc(peak_carried, 1)

                pe.wait_ge(const1, CONSTS)
                pe.wait_ge(sel_in[0], 16)
                pe.matmul(ps_cm[0:1, :], sel[:, 0:1], peak[:, :], start=True, stop=True).then_inc(peak_carried, 1)
                score(0, 0, 64)
                score(1, 1, 64)
                with pe.Fori(0, n) as i:
                    for u in range(RING):
                        s = i * RING + u
                        pe.wait_ge(prob_set, s + 1)
                        alone(pe)
                        for prob, ps in ((prob1, ps_p1), (prob2, ps_p2)):
                            for j in range(TILES):
                                ins = pe.transpose(ps[:, j * W:(j + 1) * W], prob[:, j * P:(j + 1) * P], ident[0:W, 0:W])
                            ins.then_inc(prob_turned, 1)
                        carry_peak(s + 1, (u + 1) % RING, i)
                        pe.matmul(ps_ca[0:1, 0:ZC], sel[:, u:u + 1], total[:, :], start=True, stop=True).then_inc(total_carried, 1)
                        score(s + 2, (u + 2) % RING, i * 64 + 64 * (1 + (u + 2) // RING))
                        pe.wait_ge(carried_set, s + 2)
                        pe.wait_ge(carry_set, s + 1)
                        pe.wait_ge(prob_t_set, s + 1)
                        for j in range(TILES):
                            pe.matmul(ps_o[0:W, 0:ZC], prob_t[:, j, :], rows[:, u, j, :], start=(j == 0), stop=False)
                        pe.matmul(ps_o[0:W, 0:ZC], row0[:, :], carry_in[:, :], start=False, stop=True).then_inc(summed, 1)

            @block.vector
            def _(v):
                v.sem_inc(total_set, 1)
                v.sem_inc(h_free, RING)
                v.memset(inverse[:, :], 1.0).then_inc(inverse_set, 1)
                v.memset(rows[:, :, :, Z:ZC], 1.0).then_inc(const1, 1)
                v.memset(pen_e[0:1, :, :], 1.0).then_inc(const1, 1)
                v.memset(peak[:, :], 1.0).then_inc(const1, 1)
                v.memset(carried[:, :], FLOOR)
                v.memset(total[:, :], 0.0).then_inc(const1, 1)
                v.tensor_copy(row0[:, :], ident[0:1, 0:W]).then_inc(const1, 1)
                v.wait_ge(const1, CONSTS)
                n = iterations(v)

                def logits(s, u, loads, gathered):
                    v.wait_ge(loads_in[u], loads)
                    v.tensor_tensor(product[:, :, :], edge_f[:, u, :, :],
                                    v_edge[:, :].unsqueeze(1).to_broadcast([P, TILES, K64]), ALU.mult).then_inc(product_set, 1)
                    v.wait_ge(product_set, s + 1)
                    v.tensor_reduce(edge_r[:, :], product[:, :, :], AX.X, ALU.add).then_inc(r_set, 1)
                    v.wait_ge(r_set, s + 1)
                    v.wait_ge(rows_in[u], gathered)
                    v.tensor_tensor(logit[:, u % 2, :], edge_r[:, :], rows[:, u, :, D], ALU.add).then_inc(logit_set, 1)

                def raw_peaks(s, u):
                    v.wait_ge(scored, s + 1)
                    v.tensor_reduce(top[:, :], ps_m[u % 2][:, 0:GROUP], AX.X, ALU.max).then_inc(top_set, 1)

                def weights(s, u):
                    v.wait_ge(prob_turned, s * 2 + 2)
                    v.wait_ge(prob_copied, s + 1)
                    v.tensor_tensor(prob_t[:, :, :].rearrange("p j w -> p (j w)"), prob_a[:, :],
                                    ps_p2[:, 0:TILES * W], ALU.max).then_inc(prob_t_set, 1)

                def peaks(s, u):
                    q = q_win[:, u:u + 1]
                    v.wait_ge(peak_carried, s + 1)
                    v.tensor_scalar(valid[:, :], ps_cm[0:1, 1:2], 1.0, -FLOOR, ALU.subtract, ALU.mult).then_inc(valid_set, 1)
                    v.wait_ge(top_set, s + 1)
                    v.tensor_tensor(top_q[:, :], top[:, :], q, ALU.add).then_inc(topq_set, 1)
                    v.wait_ge(valid_set, s + 1)
                    v.tensor_tensor(carried[0:1, :], valid[:, :], ps_cm[0:1, 0:1], ALU.add).then_inc(carried_set, 1)
                    v.wait_ge(topq_set, s + 1)
                    v.scalar_tensor_tensor(out=top_l[:, :], in0=top_q[:, :], scalar=0.2, in1=top_q[:, :], op0=ALU.mult,
                                           op1=ALU.max).then_inc(topl_set, 1)
                    v.wait_ge(topl_set, s + 1)
                    v.wait_ge(carried_set, s + 1)
                    v.tensor_tensor(peak[:, 0:1], top_l[:, :], carried[:, :], ALU.max).then_inc(peak_set, 1)
                    v.wait_ge(peak_set, s + 1)
                    v.tensor_tensor(bias1[:, :], q, peak[:, 0:1], ALU.subtract).then_inc(bias1_set, 1)
                    v.scalar_tensor_tensor(out=bias2[:, :], in0=q, scalar=0.2, in1=peak[:, 0:1], op0=ALU.mult,
                                           op1=ALU.subtract).then_inc(bias2_set, 1)

                logits(0, 0, 64, 80)
                logits(1, 1, 64, 80)
                raw_peaks(0, 0)
                peaks(0, 0)
                raw_peaks(1, 1)
                logits(2, 2, 64, 80)
                with v.Fori(0, n) as i:
                    for u in range(RING):
                        s = i * RING + u
                        u1, u2, u3 = ((u + k) % RING for k in (1, 2, 3))
                        turn = 1 + (u + 3) // RING
                        weights(s, u)
                        peaks(s + 1, u1)
                        logits(s + 3, u3, i * 64 + 64 * turn, i * 80 + 80 * turn)
                        raw_peaks(s + 2, u2)
                        v.wait_ge(summed, s + 2)
                        v.tensor_copy(total[:, :], ps_o[0:W, 0:ZC]).then_inc(total_set, 1)
                        v.wait_ge(total_set, s + 2)
                        s_col = total[:, ZC - 1:ZC]
                        v.scalar_tensor_tensor(out=weight[:, :], in0=s_col, scalar=0.0, in1=s_col, op0=ALU.is_equal,
                                               op1=ALU.add).then_inc(weight_set, 1)
                        v.wait_ge(weight_set, s + 1)
                        v.reciprocal(inverse[:, :], weight[:, :]).then_inc(inverse_set, 1)

        with ExitStack() as c:
            step = max(1, x_blocks // 10)
            parts = x_blocks // step
            h_in = tensor(c, "h_in", [x_part, x_blocks, D])
            h_loaded = [sem(c, f"h_loaded{t}") for t in range(parts)]
            out_set, out_stored = sem(c, "out_set"), sem(c, "out_stored")
            block = c.enter_context(nc.Block())

            @block.sync
            def _(sp):
                h_v = h_table[0:n_nodes].rearrange("(p b) d -> p b d", p=x_part)
                for t in range(parts):
                    sp.dma_start(h_in[:, t * step:(t + 1) * step, :], h_v[:, t * step:(t + 1) * step, :]).then_inc(h_loaded[t], 16)

            @block.vector
            def _(v):
                for t in range(parts):
                    v.wait_ge(h_loaded[t], 16)
                    h = h_in[:, t * step:(t + 1) * step, :]
                    v.tensor_tensor(h, h, xn[:, t * step:(t + 1) * step, :], ALU.add).then_inc(out_set, 1)

            @block.scalar
            def _(act):
                o_v = out.rearrange("(p b) d -> p b d", p=x_part)
                for t in range(parts):
                    act.wait_ge(out_set, t + 1)
                    act.dma_start(o_v[:, t * step:(t + 1) * step, :], h_in[:, t * step:(t + 1) * step, :]).then_inc(out_stored, 16)
                act.wait_ge(out_stored, 16 * parts)


_INS = ["x", "src", "dst", "edge_attr_16", "edge_attr_64", "L0_gnn_W_emb", "L0_gnn_b_emb", "L0_gnn_W_lin", "L0_gnn_b_lin",
        "L1_gnn_Wn", "L1_gnn_We", "L1_gnn_Wa"]


def kernel(**inputs):
    import numpy as np
    import concourse.bacc as bacc
    from concourse.bass_utils import run_bass_kernel_spmd

    nc = bacc.Bacc("TRN2", target_bir_lowering=False, num_devices=1)
    arrays, args = {}, []
    for name in _INS:
        a = np.ascontiguousarray(inputs[name])
        arrays[f"in_{name}"] = a
        args.append(nc.dram_tensor(f"in_{name}", a.shape, mybir.dt.from_np(a.dtype), kind="ExternalInput").ap())
    out = nc.dram_tensor("out_0", arrays["in_x"].shape, F32, kind="ExternalOutput").ap()
    bass_gnn(nc, *args, out)
    r = run_bass_kernel_spmd(nc, [arrays], core_ids=[0])
    return r.results[0]["out_0"]
```

```python
from contextlib import ExitStack

import concourse.bass as bass
from concourse import mybir

ALU = mybir.AluOpType
ACT = mybir.ActivationFunctionType
AX = mybir.AxisListType
F32 = mybir.dt.float32
BF16 = mybir.dt.bfloat16
I32 = mybir.dt.int32

P = 128
TILES = 5
GROUP = TILES * P
W = 64
DIGITS = 5
NODE_BITS = 14
ROWS = DIGITS + 2
PIECES = 2
UNITS = PIECES * DIGITS
PENALTY = 2.0 ** 110
FLOOR = -1.0e30
LN_EPS = 1e-5
CH = 5
HALF = 3
RING = 2 * HALF


def bass_gnn(nc, x, src, dst, dst_rows, ea16, ea64, w_emb, b_emb, w_lin, b_lin, wn, we, wa, out,
             q_part=125, x_part=125):
    n_nodes, D = x.shape
    n_groups, _, K16, _ = ea16.shape
    n_edges = n_groups * GROUP
    K64 = ea64.shape[1]
    H = w_emb.shape[1]
    q_blocks = n_groups // q_part
    x_blocks = n_nodes // x_part
    assert q_part * q_blocks == n_groups and x_part * x_blocks == n_nodes
    assert D == P and H == K64 and n_nodes <= 8 ** DIGITS
    assert n_nodes + W < 2 ** NODE_BITS and (n_groups + n_nodes // W) * 2 ** NODE_BITS <= 2 ** 24
    n_pad = -(-(n_nodes + 2 * W) // P) * P
    spare = n_nodes + W
    pad_part = n_pad // P
    most_steps = n_groups + n_nodes // W
    most_iter = -(-most_steps // RING)
    least_iter = -(-n_groups // RING)
    assert x_blocks <= least_iter
    x_room = max(x_blocks + 2 * CH, most_iter)
    step_cols = -(-(most_iter * RING + RING) // P)
    n_table = step_cols * P
    Z = D + 1
    ZC = D + 2

    pen_edge = nc.dram_tensor("pen_edge", (ROWS - 1, n_edges), BF16, kind="Internal").ap()
    pen_node = nc.dram_tensor("pen_node", (ROWS, n_pad), BF16, kind="Internal").ap()
    z_table = nc.dram_tensor("z_table", (n_nodes, Z), F32, kind="Internal").ap()
    q_table = nc.dram_tensor("q_table", (n_pad, 1), F32, kind="Internal").ap()
    h_table = nc.dram_tensor("h_table", (n_pad, D), F32, kind="Internal").ap()

    whole = ExitStack()

    def tensor(ctx, name, shape, dt=F32):
        return ctx.enter_context(nc.sbuf_tensor(name, shape, dt))

    def bank(ctx, name, cols=512, parts=P):
        return ctx.enter_context(nc.psum_tensor(name, [parts, cols], F32))

    def sem(ctx, name):
        return ctx.enter_context(nc.semaphore(name))

    with whole:
        eps = tensor(whole, "eps", [x_part, 1])
        ident = tensor(whole, "ident", [P, P])
        src_e = tensor(whole, "src_e", [P, n_groups * TILES], I32)
        base_f = tensor(whole, "base_f", [P, n_table])
        carry_sel = tensor(whole, "carry_sel", [P, n_table])
        step_gb = tensor(whole, "step_gb", [1, n_table], I32)
        n_iter = tensor(whole, "n_iter", [1, 1], I32)
        v_edge = tensor(whole, "v_edge", [P, K64])
        wn_x = tensor(whole, "wn_x", [P, D + 2])
        w_lin_x = tensor(whole, "w_lin_x", [H + 1, D])
        w_emb_x = tensor(whole, "w_emb_x", [P, TILES * H])
        xn = tensor(whole, "xn", [x_part, x_room, D])
        tables_done = sem(whole, "tables_done")
        waits_passed = sem(whole, "waits_passed")
        dst_e = tensor(whole, "dst_e", [P, n_groups * TILES])
        rstd0 = tensor(whole, "rstd0", [x_part, x_room])
        shift0 = tensor(whole, "shift0", [x_part, x_room])

        with ExitStack() as c:
            dst_i = tensor(c, "dst_i", [P, n_groups * TILES], I32)
            lnx = tensor(c, "lnx", [x_part, x_blocks, 6])
            mv = tensor(c, "mv", [x_part, x_blocks, 2])
            spread = tensor(c, "spread", [x_part, x_blocks])
            cols_d = n_edges // q_part // PIECES
            dst_d = tensor(c, "dst_d", [q_part, PIECES, cols_d], I32)
            digit_i = tensor(c, "digit_i", [q_part, 2, cols_d], I32)
            digit_h = tensor(c, "digit_h", [q_part, 2, cols_d], BF16)
            square_h = tensor(c, "square_h", [q_part, 2, cols_d], BF16)
            sum_h = tensor(c, "sum_h", [q_part, PIECES, cols_d], BF16)
            pen_v = pen_edge.rearrange("r (q t e) -> r t q e", q=q_part, t=PIECES)
            digit_set, squared, summed_sq, in_rows, sum_stored = (
                sem(c, n) for n in ("digit_set", "squared", "summed_sq", "in_rows", "sum_stored"))
            digit_stored = [sem(c, f"digit_stored{u}") for u in range(2)]
            node_i = tensor(c, "node_i", [pad_part, P], I32)
            nd_i = tensor(c, "nd_i", [pad_part, DIGITS, P], I32)
            nd_f = tensor(c, "nd_f", [pad_part, P])
            nd_s = tensor(c, "nd_s", [pad_part, P])
            nd_q = tensor(c, "nd_q", [pad_part, P])
            nd_h = tensor(c, "nd_h", [pad_part, ROWS, P], BF16)
            last_sel = tensor(c, "last_sel", [P, P])
            row_col = tensor(c, "row_col", [P, 1])
            step_col = tensor(c, "step_col", [P, step_cols])
            ends = tensor(c, "ends", [P, n_groups + 1])
            starts = tensor(c, "starts", [P, n_groups + 1])
            span_f = tensor(c, "span_f", [P, n_groups])
            span_i = tensor(c, "span_i", [P, n_groups], I32)
            quotient = tensor(c, "quotient", [P, n_groups])
            left = tensor(c, "left", [P, n_groups])
            ones_g = tensor(c, "ones_g", [P, n_groups])
            found = tensor(c, "found", [P, n_groups])
            start_end = tensor(c, "start_end", [P, n_groups])
            packed = tensor(c, "packed", [P, step_cols], I32)
            part_i = tensor(c, "part_i", [P, step_cols], I32)
            got = tensor(c, "got", [P, 4, step_cols])
            sb_f = tensor(c, "sb_f", [P, step_cols])
            sg_f = tensor(c, "sg_f", [P, step_cols])
            spare_f = tensor(c, "spare_f", [P, step_cols])
            wide_f = tensor(c, "wide_f", [P, n_table])
            iter_row = tensor(c, "iter_row", [1, most_iter])
            begun = tensor(c, "begun", [1, most_iter])
            iter_f = tensor(c, "iter_f", [1, 1])
            zero_rows = tensor(c, "zero_rows", [P, D])
            wn_nat = tensor(c, "wn_nat", [P, D])
            wa_col = tensor(c, "wa_col", [P, 3])
            we_nat = tensor(c, "we_nat", [P, K64])
            groups = bank(c, "groups", 1024)
            wide = bank(c, "wide", 1024)
            small = bank(c, "small")
            in_dst, in_src = sem(c, "in_dst"), sem(c, "in_src")
            in_w, in_wdiag, in_x = sem(c, "in_w"), sem(c, "in_wdiag"), sem(c, "in_x")
            p_const, p_ident, v_zero = sem(c, "p_const"), sem(c, "p_ident"), sem(c, "v_zero")
            v_nat, v_chain, t_small, t_wide = sem(c, "v_nat"), sem(c, "v_chain"), sem(c, "t_small"), sem(c, "t_wide")
            ln_stat, ln_aggr, ln_root, p_chain, v_nodes = (
                sem(c, n) for n in ("ln_stat", "ln_aggr", "ln_root", "p_chain", "v_nodes"))
            p_node, d_node, d_zero, v_cols = sem(c, "p_node"), sem(c, "d_node"), sem(c, "d_zero"), sem(c, "v_cols")
            block = c.enter_context(nc.Block())

            @block.sync
            def _(sp):
                sp.dma_start(dst_i[:, :], dst.rearrange("p g j -> p (g j)")).then_inc(in_dst, 16)
                sp.dma_start(xn[:, 0:x_blocks, :], x.rearrange("(p b) d -> p b d", p=x_part)).then_inc(in_x, 16)
                sp.dma_start(dst_d[:, :, :].rearrange("q t e -> q (t e)"),
                             dst_rows.rearrange("(q b) j p -> q (b j p)", q=q_part)).then_inc(in_rows, 16)
                sp.dma_start(src_e[:, :], src.rearrange("p g j -> p (g j)")).then_inc(in_src, 16)
                sp.wait_ge(v_zero, 2)
                for j in range(TILES):
                    sp.dma_start(w_emb_x[1 + j * K16:1 + (j + 1) * K16, j * H:(j + 1) * H], w_emb).then_inc(in_wdiag, 16)
                    sp.dma_start(w_emb_x[0:1, j * H:(j + 1) * H],
                                 b_emb.rearrange("(a n) -> a n", a=1)).then_inc(in_wdiag, 16)
                sp.dma_start(h_table.rearrange("(p r) d -> p r d", p=P),
                             zero_rows[:, :].unsqueeze(1).to_broadcast([P, pad_part, D])).then_inc(d_zero, 16)
                for n in range(UNITS):
                    t, k = divmod(n, DIGITS)
                    sp.wait_ge(squared, n + 1)
                    sp.dma_start(pen_v[1 + k, t], digit_h[:, n % 2, :]).then_inc(digit_stored[n % 2], 16)
                    if k == DIGITS - 1:
                        sp.wait_ge(summed_sq, n + 1)
                        sp.dma_start(pen_v[0, t], sum_h[:, t, :]).then_inc(sum_stored, 16)
                sp.wait_ge(p_node, 1)
                for k in range(ROWS):
                    sp.dma_start(pen_node[k].rearrange("(p r) -> p r", r=P), nd_h[:, k, :]).then_inc(d_node, 16)
                sp.wait_ge(in_wdiag, 16 * 2 * TILES)
                sp.wait_ge(d_zero, 16)
                sp.wait_ge(in_src, 16)
                sp.wait_ge(sum_stored, 16 * PIECES)
                for u in range(2):
                    sp.wait_ge(digit_stored[u], 16 * (UNITS // 2))
                sp.wait_ge(d_node, 16 * ROWS)
                sp.wait_ge(in_x, 16)

            @block.gpsimd
            def _(pool):
                pool.memset(ident[:, :], 0.0).then_inc(p_ident, 1)
                pool.memset(last_sel[:, :], 0.0).then_inc(p_ident, 1)
                pool.wait_ge(p_ident, 2)
                pool.affine_select(out=ident[:, :], in_=ident[:, :], compare_op=ALU.not_equal, fill=1.0, base=0,
                                   pattern=[[-1, P]], channel_multiplier=1).then_inc(p_const, 1)
                pool.affine_select(out=last_sel[:, :], in_=last_sel[:, :], compare_op=ALU.not_equal, fill=1.0,
                                   base=1 - P, pattern=[[0, P]], channel_multiplier=1).then_inc(p_const, 1)
                pool.iota(row_col[:, :], [[0, 1]], 0, 1, allow_small_or_imprecise_dtypes=True).then_inc(p_const, 1)
                pool.iota(step_col[:, :], [[P, step_cols]], 0, 1, allow_small_or_imprecise_dtypes=True).then_inc(p_const, 1)
                pool.iota(node_i[:, :], [[1, P]], 0, P).then_inc(p_const, 1)
                pool.iota(iter_row[:, :], [[RING, most_iter]], 0, 1, allow_small_or_imprecise_dtypes=True).then_inc(p_const, 1)
                pool.memset(xn[:, x_blocks:x_room, :], 0.0)
                chain = [0]

                def then(ins):
                    chain[0] += 1
                    ins.then_inc(p_chain, 1)
                    pool.wait_ge(p_chain, chain[0])

                pool.wait_ge(v_nodes, DIGITS)
                for k in range(DIGITS):
                    then(pool.tensor_copy(nd_f[:, :], nd_i[:, k, :]))
                    then(pool.tensor_scalar(nd_h[:, 2 + k, :], nd_f[:, :], 2.0 * PENALTY, None, ALU.mult))
                    if k == 0:
                        then(pool.tensor_tensor(nd_s[:, :], nd_f[:, :], nd_f[:, :], ALU.mult))
                    else:
                        then(pool.tensor_tensor(nd_q[:, :], nd_f[:, :], nd_f[:, :], ALU.mult))
                        then(pool.tensor_tensor(nd_s[:, :], nd_s[:, :], nd_q[:, :], ALU.add))
                then(pool.memset(nd_h[:, 1, :], -PENALTY))
                pool.tensor_scalar(nd_h[:, 0, :], nd_s[:, :], -PENALTY, None, ALU.mult).then_inc(p_node, 1)
                for n in range(UNITS):
                    t, k = divmod(n, DIGITS)
                    pool.wait_ge(squared, n + 1)
                    if k == 0:
                        pool.tensor_copy(sum_h[:, t, :], square_h[:, n % 2, :]).then_inc(summed_sq, 1)
                    else:
                        pool.wait_ge(summed_sq, n)
                        pool.tensor_tensor(sum_h[:, t, :], sum_h[:, t, :], square_h[:, n % 2, :], ALU.add).then_inc(summed_sq, 1)

            @block.scalar
            def _(act):
                act.dma_start(wn_nat[:, :], wn).then_inc(in_w, 16)
                act.dma_start(we_nat[:, :], we).then_inc(in_w, 16)
                for k in range(3):
                    act.dma_start(wa_col[:, k:k + 1], wa[:, k * D:(k + 1) * D].rearrange("a d -> d a")).then_inc(in_w, 16)
                act.dma_start(w_lin_x[0:H, :], w_lin).then_inc(in_w, 16)
                act.dma_start(w_lin_x[H:H + 1, :], b_lin.rearrange("(a n) -> a n", a=1)).then_inc(in_w, 16)
                for n in range(UNITS):
                    act.wait_ge(digit_set, n + 1)
                    if n >= 2:
                        act.wait_ge(digit_stored[n % 2], 16 * (n // 2))
                        act.wait_ge(summed_sq, n - 1)
                    act.activation(digit_h[:, n % 2, :], digit_i[:, n % 2, :], ACT.Copy)
                    act.activation(square_h[:, n % 2, :], digit_i[:, n % 2, :], ACT.Square).then_inc(squared, 1)
                act.wait_ge(ln_aggr, x_blocks)
                act.activation(spread[:, :], mv[:, :, 1], ACT.Sqrt, bias=eps[:, :]).then_inc(ln_root, 1)
                act.wait_ge(in_w, 112)

            @block.tensor
            def _(pe):
                pe.wait_ge(p_const, 2)
                pe.wait_ge(v_nat, 1)
                ends_in = dst_e[:, TILES - 1::TILES]
                for lo in range(0, n_groups, 512):
                    hi = min(lo + 512, n_groups)
                    ins = pe.matmul(wide[:, lo:hi], last_sel[:, :], ends_in[:, lo:hi], start=True, stop=True)
                ins.then_inc(t_wide, 1)
                pe.wait_ge(in_w, 112)
                pe.transpose(small[:, 0:D], wn_nat[:, :], ident[:, :])
                pe.matmul(small[:, D:D + 2], wn_nat[:, :], wa_col[:, 0:2], start=True, stop=True)
                pe.matmul(small[:, 256:256 + K64], wa_col[:, 2:3].to_broadcast([P, P]), we_nat[:, :],
                          start=True, stop=True).then_inc(t_small, 1)
                pe.wait_ge(v_cols, 1)
                for k in range(step_cols):
                    ins = pe.matmul(wide[:, k * P:(k + 1) * P], sb_f[:, k:k + 1].to_broadcast([P, P]), ident[:, :],
                                    start=True, stop=True)
                ins.then_inc(t_wide, 1)
                for k in range(step_cols):
                    ins = pe.matmul(groups[:, k * P:(k + 1) * P], sg_f[:, k:k + 1].to_broadcast([P, P]), ident[:, :],
                                    start=True, stop=True)
                ins.then_inc(t_wide, 1)

            @block.vector
            def _(v):
                chain = [0]

                def then(ins):
                    chain[0] += 1
                    ins.then_inc(v_chain, 1)
                    v.wait_ge(v_chain, chain[0])

                v.memset(w_emb_x[:, :], 0.0).then_inc(v_zero, 1)
                v.memset(zero_rows[:, :], 0.0).then_inc(v_zero, 1)
                v.memset(ones_g[:, :], 1.0)
                v.memset(eps[:, :], LN_EPS)
                v.memset(ends[:, 0:1], 0.0)
                then(v.memset(starts[:, 0:1], 0.0))
                v.memset(rstd0[:, :], 0.0)
                v.memset(shift0[:, :], 0.0)
                v.wait_ge(p_const, 6)
                for k in range(DIGITS):
                    v.tensor_scalar(nd_i[:, k, :], node_i[:, :], 3 * k, 7, ALU.arith_shift_right, ALU.bitwise_and).then_inc(v_nodes, 1)
                v.wait_ge(in_dst, 16)
                v.tensor_copy(dst_e[:, :], dst_i[:, :]).then_inc(v_nat, 1)
                v.wait_ge(t_wide, 1)
                then(v.tensor_copy(ends[:, 1:n_groups + 1], wide[:, 0:n_groups]))
                then(v.tensor_tensor(span_f[:, :], ends[:, 1:n_groups + 1], ends[:, 0:n_groups], ALU.subtract))
                then(v.tensor_scalar(span_i[:, :], span_f[:, :], 1.0 / W, None, ALU.mult))
                then(v.tensor_copy(quotient[:, :], span_i[:, :]))
                then(v.scalar_tensor_tensor(out=left[:, :], in0=quotient[:, :], scalar=-float(W), in1=span_f[:, :],
                                            op0=ALU.mult, op1=ALU.add))
                then(v.tensor_scalar(span_f[:, :], left[:, :], 0.0, -1.0, ALU.is_lt, ALU.mult))
                then(v.tensor_tensor(quotient[:, :], quotient[:, :], span_f[:, :], ALU.add))
                then(v.tensor_scalar(left[:, :], left[:, :], float(W), None, ALU.is_ge))
                then(v.tensor_tensor(span_f[:, :], quotient[:, :], left[:, :], ALU.add))
                then(v.tensor_tensor_scan(starts[:, 1:n_groups + 1], span_f[:, :], ones_g[:, :], 0.0, ALU.add, ALU.add))
                then(v.tensor_scalar(begun[:, :], iter_row[:, :], starts[0:1, n_groups:n_groups + 1], None, ALU.is_lt))
                then(v.tensor_reduce(iter_f[:, :], begun[:, :], AX.X, ALU.add))
                then(v.tensor_copy(n_iter[:, :], iter_f[:, :]))
                v.wait_ge(in_rows, 16)

                def digit(n):
                    t, k = divmod(n, DIGITS)
                    if n >= 2:
                        v.wait_ge(squared, n - 1)
                    v.tensor_scalar(digit_i[:, n % 2, :], dst_d[:, t, :], 3 * k, 7, ALU.arith_shift_right,
                                    ALU.bitwise_and).then_inc(digit_set, 1)

                then(v.scalar_tensor_tensor(out=start_end[:, :], in0=starts[:, 0:n_groups], scalar=float(2 ** NODE_BITS),
                                            in1=ends[:, 0:n_groups], op0=ALU.mult, op1=ALU.add))
                for k in range(step_cols):
                    for n in range(k * UNITS // step_cols, (k + 1) * UNITS // step_cols):
                        digit(n)
                    s = step_col[:, k:k + 1]
                    then(v.tensor_scalar(found[:, :], starts[:, 0:n_groups], s, None, ALU.is_le))
                    then(v.tensor_reduce(got[:, 0, k:k + 1], found[:, :], AX.X, ALU.add))
                    then(v.scalar_tensor_tensor(out=found[:, :], in0=starts[:, 0:n_groups], scalar=s,
                                                in1=start_end[:, :], op0=ALU.is_le, op1=ALU.mult))
                    then(v.tensor_reduce(got[:, 1, k:k + 1], found[:, :], AX.X, ALU.max))
                then(v.tensor_copy(packed[:, :], got[:, 1, :]))
                then(v.tensor_scalar(part_i[:, :], packed[:, :], NODE_BITS, None, ALU.arith_shift_right))
                then(v.tensor_copy(got[:, 1, :], part_i[:, :]))
                then(v.tensor_scalar(part_i[:, :], packed[:, :], 2 ** NODE_BITS - 1, None, ALU.bitwise_and))
                then(v.tensor_copy(got[:, 2, :], part_i[:, :]))
                then(v.tensor_scalar(sg_f[:, :], got[:, 0, :], 1.0, None, ALU.subtract))
                then(v.tensor_tensor(got[:, 3, :], step_col[:, :], got[:, 1, :], ALU.subtract))
                then(v.scalar_tensor_tensor(out=sb_f[:, :], in0=got[:, 3, :], scalar=float(W), in1=got[:, 2, :],
                                            op0=ALU.mult, op1=ALU.add))
                then(v.tensor_scalar(spare_f[:, :], step_col[:, :], starts[:, n_groups:n_groups + 1], None, ALU.is_ge))
                then(v.tensor_scalar(got[:, 3, :], sb_f[:, :], -1.0, float(spare), ALU.mult, ALU.add))
                then(v.tensor_tensor(got[:, 3, :], got[:, 3, :], spare_f[:, :], ALU.mult))
                v.tensor_tensor(sb_f[:, :], sb_f[:, :], got[:, 3, :], ALU.add).then_inc(v_cols, 1)
                v.wait_ge(t_small, 1)
                v.tensor_copy(wn_x[:, :], small[:, 0:D + 2])
                v.tensor_copy(v_edge[:, :], small[:, 256:256 + K64])
                v.wait_ge(in_x, 16)
                for b in range(x_blocks):
                    v.bn_stats(lnx[:, b, :], xn[:, b, :]).then_inc(ln_stat, 1)
                for b in range(x_blocks):
                    v.wait_ge(ln_stat, b + 1)
                    v.bn_aggr(mv[:, b, :], lnx[:, b, :]).then_inc(ln_aggr, 1)
                v.wait_ge(t_wide, 2)
                then(v.tensor_copy(base_f[:, :], wide[:, 0:n_table]))
                then(v.tensor_tensor(wide_f[:, 1:n_table], base_f[:, 1:n_table], base_f[:, 0:n_table - 1], ALU.subtract))
                then(v.memset(wide_f[:, 0:1], -1.0))
                then(v.tensor_scalar(carry_sel[:, :], wide_f[:, :], row_col[:, 0:1], None, ALU.is_equal))
                v.wait_ge(t_wide, 3)
                v.scalar_tensor_tensor(out=step_gb[:, :], in0=groups[0:1, 0:n_table], scalar=float(2 ** NODE_BITS),
                                       in1=base_f[0:1, :], op0=ALU.mult, op1=ALU.add).then_inc(tables_done, 1)
                v.wait_ge(ln_root, 1)
                then(v.reciprocal(rstd0[:, 0:x_blocks], spread[:, :]))
                v.scalar_tensor_tensor(out=shift0[:, 0:x_blocks], in0=mv[:, :, 0], scalar=-1.0, in1=rstd0[:, 0:x_blocks],
                                       op0=ALU.mult, op1=ALU.mult).then_inc(tables_done, 1)
                v.wait_ge(tables_done, 2)

        KT = TILES * K16
        last_g = n_groups - 1

        def iterations(eng):
            return eng.value_load(n_iter[0:1, 0:1], min_val=-(-n_groups // RING), max_val=most_iter)

        def alone(eng):
            eng.sem_inc(waits_passed, 1)

        def steps_from(engine, s, count):
            loaded = nc.values_load_multi_w_load_instructions(
                step_gb[0:1, bass.ds(s, count)], engines=[engine], min_val=0, max_val=last_g * 2 ** NODE_BITS + spare)
            return loaded[1]

        def group_of(eng, entry):
            return nc.s_assert_within(eng.snap(entry >> NODE_BITS), 0, last_g,
                                      skip_runtime_bounds_check_because="the table holds groups")

        def base_of(eng, entry):
            return nc.s_assert_within(eng.snap(entry & (2 ** NODE_BITS - 1)), 0, spare,
                                      skip_runtime_bounds_check_because="the table holds windows")

        with ExitStack() as layer0:
            acc = tensor(layer0, "acc", [H + 1, n_pad])
            with ExitStack() as c:
                h0 = tensor(c, "h0", [x_part, D])
                ea = tensor(c, "ea", [P, RING, P])
                offs = tensor(c, "offs", [P, RING, TILES])
                cols = tensor(c, "cols", [P, TILES, W])
                hot = tensor(c, "hot", [P, RING, TILES, W])
                hid = tensor(c, "hid", [P, 2, TILES, H + 1])
                ps_u = [bank(c, f"ps_u{i}") for i in range(2)]
                ps_s = [bank(c, f"ps_s{i}") for i in range(RING)]
                ea_in = [sem(c, f"ea_in{u}") for u in range(RING)]
                const0, zeroed = sem(c, "const0"), sem(c, "zeroed")
                embedded, activated, summed, added = (
                    sem(c, n) for n in ("embedded", "activated", "summed", "added"))
                offset_set, hot_set = sem(c, "offset_set"), sem(c, "hot_set")
                ea_zero = sem(c, "ea_zero")
                h0_set, h0_added = sem(c, "h0_set"), sem(c, "h0_added")
                block = c.enter_context(nc.Block())

                @block.sync
                def _(sp):
                    n = iterations(sp)
                    sp.wait_ge(ea_zero, 1)

                    def load(entry, u):
                        g = group_of(sp, entry)
                        sp.dma_start(ea[1:1 + KT, u, :], ea16[bass.ds(g, 1)].rearrange("a j k p -> (a j k) p")).then_inc(ea_in[u], 16)

                    first = steps_from(mybir.EngineType.SP, 0, RING)
                    for u in range(RING):
                        load(first[u], u)
                    with sp.Fori(0, n) as i:
                        ahead = steps_from(mybir.EngineType.SP, i * RING + RING, RING)
                        for u in range(RING):
                            sp.wait_ge(embedded, i * RING + (u + 1))
                            alone(sp)
                            load(ahead[u], u)
                    for u in range(RING):
                        sp.wait_ge(ea_in[u], n * 16 + 16)
                        alone(sp)

                @block.gpsimd
                def _(pool):
                    pool.iota(cols[:, :, :], [[0, TILES], [1, W]], 0, 0, allow_small_or_imprecise_dtypes=True).then_inc(const0, 1)
                    n = iterations(pool)

                    def offset(entry, s, u):
                        g = group_of(pool, entry)
                        pool.tensor_tensor(offs[:, u, :], dst_e[:, bass.ds(g * TILES, TILES)],
                                           base_f[:, bass.ds(s, 1)].to_broadcast([P, TILES]), ALU.subtract).then_inc(offset_set, 1)

                    first = steps_from(mybir.EngineType.Pool, 0, RING)
                    for u in range(RING):
                        offset(first[u], u, u)
                    pool.memset(acc[:, n_pad // 2:n_pad], 0.0).then_inc(zeroed, 1)
                    with pool.Fori(0, n) as i:
                        ahead = steps_from(mybir.EngineType.Pool, i * RING + RING, RING)
                        for u in range(RING):
                            pool.wait_ge(hot_set, i * RING + (u + 1))
                            offset(ahead[u], i * RING + (u + RING), u)
                        pool.wait_ge(h0_set, i + 1)
                        alone(pool)
                        block_x = xn[:, bass.ds(i, 1), :].rearrange("p a d -> p (a d)")
                        pool.tensor_tensor(block_x, block_x, h0[:, :], ALU.add).then_inc(h0_added, 1)

                @block.scalar
                def _(act):
                    n = iterations(act)

                    def silu(s, u):
                        act.wait_ge(embedded, s + 1)
                        act.activation(hid[:, u % 2, :, 0:H], ps_u[u % 2][:, 0:TILES * H].rearrange("p (j h) -> p j h", j=TILES),
                                       ACT.Silu).then_inc(activated, 1)

                    act.wait_ge(const0, 3)
                    silu(0, 0)
                    with act.Fori(0, n) as i:
                        for u in range(RING):
                            s = i * RING + u
                            act.wait_ge(summed, s + 1)
                            silu(s + 1, u + 1)
                        act.wait_ge(h0_added, i + 1)
                        alone(act)
                        act.activation(h0[:, :], xn[:, bass.ds(i, 1), :].rearrange("p a d -> p (a d)"), ACT.Relu,
                                       bias=shift0[:, bass.ds(i, 1)], scale=rstd0[:, bass.ds(i, 1)]).then_inc(h0_set, 1)

                @block.tensor
                def _(pe):
                    n = iterations(pe)
                    pe.sem_inc(summed, 1)

                    def embed(s, u, count):
                        pe.wait_ge(ea_in[u], count)
                        alone(pe)
                        pe.matmul(ps_u[u % 2][:, 0:TILES * H], ea[:, u, :], w_emb_x[:, :], start=True,
                                  stop=True).then_inc(embedded, 1)

                    def sum_up(s, u):
                        pe.wait_ge(activated, s + 1)
                        pe.wait_ge(hot_set, s + 1)
                        pe.wait_ge(added, s + 1)
                        for j in range(TILES):
                            ins = pe.matmul(ps_s[u][0:H + 1, 0:W], hid[:, u % 2, j, :], hot[:, u, j, :],
                                            start=(j == 0), stop=(j == TILES - 1))
                        ins.then_inc(summed, 1)

                    pe.wait_ge(const0, 3)
                    embed(0, 0, 16)
                    with pe.Fori(0, n) as i:
                        for u in range(RING):
                            s = i * RING + u
                            embed(s + 1, (u + 1) % RING, i * 16 + 16 * (1 + (u + 1) // RING))
                            sum_up(s, u)

                @block.vector
                def _(v):
                    v.sem_inc(added, RING)
                    v.sem_inc(h0_added, 1)
                    v.memset(ea[:, :, :], 0.0).then_inc(ea_zero, 1)
                    v.wait_ge(ea_zero, 1)
                    v.memset(ea[0:1, :, :], 1.0).then_inc(const0, 1)
                    v.memset(hid[:, :, :, H:H + 1], 1.0).then_inc(const0, 1)
                    v.wait_ge(const0, 3)
                    n = iterations(v)

                    def one_hot(s, u):
                        v.wait_ge(offset_set, s + 1)
                        v.tensor_tensor(hot[:, u % RING], cols[:, :, :],
                                        offs[:, u % RING, :].unsqueeze(2).to_broadcast([P, TILES, W]),
                                        ALU.is_equal).then_inc(hot_set, 1)

                    for u in range(HALF):
                        one_hot(u, u)
                    v.memset(acc[:, 0:n_pad // 2], 0.0).then_inc(zeroed, 1)
                    v.wait_ge(zeroed, 2)
                    with v.Fori(0, n) as i:
                        steps = steps_from(mybir.EngineType.DVE, i * RING, RING)
                        for u in range(RING):
                            s = i * RING + u
                            one_hot(s + HALF, u + HALF)
                            b = base_of(v, steps[u])
                            v.wait_ge(summed, s + 2)
                            v.wait_ge(added, s + RING)
                            v.tensor_tensor(acc[:, bass.ds(b, W)], acc[:, bass.ds(b, W)], ps_s[u][0:H + 1, 0:W],
                                            ALU.add).then_inc(added, 1)

            chunks = x_blocks // CH
            UNROLL = 4 if chunks % 4 == 0 else 2
            assert chunks * CH == x_blocks and chunks % UNROLL == 0
            rstd = tensor(layer0, "rstd1", [x_part, x_blocks + 2 * CH])
            shift = tensor(layer0, "shift1", [x_part, x_blocks + 2 * CH])
            with ExitStack() as c:
                stats = tensor(c, "stats", [x_part, x_blocks, 6])
                mv = tensor(c, "mv1", [x_part, x_blocks, 2])
                spread = tensor(c, "spread1", [x_part, x_blocks])
                acc_n = tensor(c, "acc_n", [H + 1, 2, CH, x_part])
                ps_x = [bank(c, f"ps_x{i}", 1024) for i in range(2)]
                acc_copied, x1_sum, x1_set, stat_set, mv_set, spread_set, rstd_set, shift_set = (
                    sem(c, n) for n in ("acc_copied", "x1_sum", "x1_set", "stat_set", "mv_set", "spread_set", "rstd_set",
                                        "shift_set"))
                block = c.enter_context(nc.Block())
                run = (x_part - 1) * x_blocks + 1

                @block.scalar
                def _(act):
                    with act.Fori(0, chunks // UNROLL) as i:
                        for u in range(UNROLL):
                            t = i * UNROLL + u
                            act.wait_ge(x1_sum, t + 1)
                            for k in range(CH):
                                ins = act.activation(acc_n[:, u % 2, k, :].unsqueeze(2),
                                                     acc[:, bass.ds(t * CH + k, run)][:, 0:run:x_blocks].unsqueeze(2), ACT.Copy)
                            ins.then_inc(acc_copied, 1)
                    act.wait_ge(mv_set, x_blocks)
                    act.activation(spread[:, :], mv[:, :, 1], ACT.Sqrt, bias=eps[:, :]).then_inc(spread_set, 1)

                @block.tensor
                def _(pe):
                    pe.sem_inc(x1_sum, 2)
                    with pe.Fori(0, chunks // UNROLL) as i:
                        for u in range(UNROLL):
                            t = i * UNROLL + u
                            pe.wait_ge(acc_copied, t + 1)
                            pe.wait_ge(x1_set, t + 1)
                            alone(pe)
                            for k in range(CH):
                                ins = pe.matmul(ps_x[u % 2][0:x_part, k * D:(k + 1) * D], acc_n[:, u % 2, k, :], w_lin_x[:, :],
                                                start=True, stop=True)
                            ins.then_inc(x1_sum, 1)

                @block.vector
                def _(v):
                    v.sem_inc(x1_set, 2)
                    v.memset(rstd[:, x_blocks:x_blocks + 2 * CH], 0.0)
                    v.memset(shift[:, x_blocks:x_blocks + 2 * CH], 0.0)
                    with v.Fori(0, chunks // UNROLL) as i:
                        for u in range(UNROLL):
                            t = i * UNROLL + u
                            v.wait_ge(x1_sum, t + 3)
                            xs = xn[:, bass.ds(t * CH, CH), :]
                            v.tensor_tensor(xs, xs, ps_x[u % 2][0:x_part, 0:CH * D].rearrange("p (k d) -> p k d", k=CH),
                                            ALU.add).then_inc(x1_set, 1)
                            v.wait_ge(x1_set, t + 3)
                            alone(v)
                            for k in range(CH):
                                v.bn_stats(stats[:, bass.ds(t * CH + k, 1), :].rearrange("p a d -> p (a d)"),
                                           xn[:, bass.ds(t * CH + k, 1), :].rearrange("p a d -> p (a d)")).then_inc(stat_set, 1)
                    v.wait_ge(stat_set, x_blocks)
                    for b in range(x_blocks):
                        v.bn_aggr(mv[:, b, :], stats[:, b, :]).then_inc(mv_set, 1)
                    v.wait_ge(spread_set, 1)
                    v.reciprocal(rstd[:, 0:x_blocks], spread[:, :]).then_inc(rstd_set, 1)
                    v.wait_ge(rstd_set, 1)
                    v.scalar_tensor_tensor(out=shift[:, 0:x_blocks], in0=mv[:, :, 0], scalar=-1.0, in1=rstd[:, 0:x_blocks],
                                           op0=ALU.mult, op1=ALU.mult).then_inc(shift_set, 1)
                    v.wait_ge(shift_set, 1)

            with ExitStack() as c:
                BY_V = 3
                Q = D + 2
                TOP = 512 // Q
                scaled = tensor(c, "scaled", [x_part, UNROLL, CH, D])
                h1_t = tensor(c, "h1_t", [D, 2, CH, x_part])
                z_out = tensor(c, "z_out", [x_part, UNROLL, CH, Q])
                q_out = tensor(c, "q_out", [x_part, x_blocks])
                q_zero = tensor(c, "q_zero", [1, n_pad - n_nodes])
                ps_h = [bank(c, f"ps_h{i}", 1024) for i in range(2)]
                ps_z = [bank(c, f"ps_z{i}", 1024) for i in range(2)]
                scaled_v, scaled_a, h1_turned, h1_set, z_sum, z_set, q_set = (
                    sem(c, n) for n in ("scaled_v", "scaled_a", "h1_turned", "h1_set", "z_sum", "z_set", "q_set"))
                z_stored = [sem(c, f"z_stored{u}") for u in range(UNROLL)]
                q_stored, q_zeroed = sem(c, "q_stored"), sem(c, "q_zeroed")
                block = c.enter_context(nc.Block())

                @block.sync
                def _(sp):
                    z_v = z_table.rearrange("(p b) c -> p b c", p=x_part)
                    with sp.Fori(0, chunks // UNROLL) as i:
                        for u in range(UNROLL):
                            t = i * UNROLL + u
                            sp.wait_ge(z_set, t + 3)
                            sp.dma_start(z_v[:, bass.ds(t * CH, CH), :], z_out[:, u, :, 0:Z]).then_inc(z_stored[u], 16)
                    for u in range(UNROLL):
                        sp.wait_ge(z_stored[u], 16 * (chunks // UNROLL + 1))
                    sp.wait_ge(q_set, chunks + UNROLL)
                    sp.wait_ge(q_zeroed, 1)
                    sp.dma_start(q_table[0:n_nodes].rearrange("(p b) c -> p (b c)", p=x_part), q_out[:, :]).then_inc(q_stored, 16)
                    sp.dma_start(q_table[n_nodes:n_pad].rearrange("n a -> a n"), q_zero[:, :]).then_inc(q_stored, 16)
                    sp.wait_ge(q_stored, 32)

                @block.gpsimd
                def _(pool):
                    pool.sem_inc(q_set, UNROLL)
                    with pool.Fori(0, chunks // UNROLL) as i:
                        for u in range(UNROLL):
                            t = i * UNROLL + u
                            pool.wait_ge(z_set, t + 3)
                            alone(pool)
                            pool.tensor_copy(q_out[:, bass.ds(t * CH, CH)], z_out[:, u, :, D + 1]).then_inc(q_set, 1)

                @block.scalar
                def _(act):
                    def scale(t, u):
                        act.wait_ge(h1_turned, t + 1)
                        for k in range(BY_V, CH):
                            b = t * CH + k
                            ins = act.activation(scaled[:, u % UNROLL, k, :], xn[:, bass.ds(b, 1), :].rearrange("p a d -> p (a d)"),
                                                 ACT.Identity, bias=shift[:, bass.ds(b, 1)], scale=rstd[:, bass.ds(b, 1)])
                        ins.then_inc(scaled_a, 1)

                    scale(0, 0)
                    scale(1, 1)
                    with act.Fori(0, chunks // UNROLL) as i:
                        for u in range(UNROLL):
                            t = i * UNROLL + u
                            scale(t + 2, u + 2)
                            act.wait_ge(h1_turned, t + (UNROLL + 1))
                            act.wait_ge(z_sum, t + 1)
                            act.activation(h1_t[:, u % 2, :, :], ps_h[u % 2][:, 0:CH * P].rearrange("p (k n) -> p k n", k=CH)[:, :, 0:x_part],
                                           ACT.Relu).then_inc(h1_set, 1)

                @block.tensor
                def _(pe):
                    pe.sem_inc(h1_turned, UNROLL)
                    pe.sem_inc(z_sum, 2)

                    def products(t, u):
                        pe.wait_ge(h1_set, t + 1)
                        pe.wait_ge(z_set, t + 1)
                        alone(pe)
                        for k in range(CH):
                            at = k * Q if k < TOP else 512 + (k - TOP) * Q
                            ins = pe.matmul(ps_z[u % 2][0:x_part, at:at + Q], h1_t[:, u % 2, k, :], wn_x[:, :],
                                            start=True, stop=True)
                        ins.then_inc(z_sum, 1)

                    def turns(t, u):
                        pe.wait_ge(scaled_v, t + 1)
                        pe.wait_ge(scaled_a, t + 1)
                        for k in range(CH):
                            ins = pe.transpose(ps_h[u % 2][:, k * P:k * P + x_part], scaled[:, u % UNROLL, k, :],
                                               ident[0:x_part, 0:x_part])
                        ins.then_inc(h1_turned, 1)

                    turns(0, 0)
                    with pe.Fori(0, chunks // UNROLL) as i:
                        for u in range(UNROLL):
                            turns(i * UNROLL + (u + 1), u + 1)
                            products(i * UNROLL + u, u)

                @block.vector
                def _(v):
                    v.memset(q_zero[:, :], 0.0).then_inc(q_zeroed, 1)
                    v.sem_inc(z_set, 2)
                    for u in range(UNROLL):
                        v.sem_inc(z_stored[u], 16)

                    def scale(t, u):
                        v.wait_ge(h1_turned, t + 1)
                        for k in range(BY_V):
                            b = t * CH + k
                            ins = v.tensor_scalar(scaled[:, u % UNROLL, k, :], xn[:, bass.ds(b, 1), :].rearrange("p a d -> p (a d)"),
                                                  rstd[:, bass.ds(b, 1)], shift[:, bass.ds(b, 1)], ALU.mult, ALU.add)
                        ins.then_inc(scaled_v, 1)

                    scale(0, 0)
                    scale(1, 1)
                    with v.Fori(0, chunks // UNROLL) as i:
                        for u in range(UNROLL):
                            t = i * UNROLL + u
                            scale(t + 2, u + 2)
                            v.wait_ge(z_sum, t + 3)
                            v.wait_ge(z_stored[u], i * 16 + 16)
                            v.wait_ge(q_set, t + 1)
                            alone(v)
                            v.tensor_copy(z_out[:, u, 0:TOP, :], ps_z[u % 2][0:x_part, 0:TOP * Q].rearrange("p (k q) -> p k q", k=TOP))
                            v.tensor_copy(z_out[:, u, TOP:CH, :],
                                          ps_z[u % 2][0:x_part, 512:512 + (CH - TOP) * Q].rearrange("p (k q) -> p k q", k=CH - TOP)
                                          ).then_inc(z_set, 1)

        with ExitStack() as c:
            edge_f = tensor(c, "edge_f", [P, RING, TILES, K64])
            index = tensor(c, "index", [P, RING, TILES], I32)
            rows = tensor(c, "rows", [P, RING, TILES, ZC])
            pen_e = tensor(c, "pen_e", [ROWS, RING, GROUP], BF16)
            pen_n = tensor(c, "pen_n", [ROWS, RING, W], BF16)
            q_win = tensor(c, "q_win", [W, RING])
            sel = tensor(c, "sel", [W, RING])
            product = tensor(c, "product", [P, TILES, K64])
            edge_r = tensor(c, "edge_r", [P, TILES])
            logit = tensor(c, "logit", [P, 2, TILES])
            top = tensor(c, "top", [W, 1])
            top_q = tensor(c, "top_q", [W, 1])
            top_l = tensor(c, "top_l", [W, 1])
            peak = tensor(c, "peak", [W, 2])
            carried = tensor(c, "carried", [W, 1])
            bias1 = tensor(c, "bias1", [W, 1])
            bias2 = tensor(c, "bias2", [W, 1])
            valid = tensor(c, "valid", [1, 1])
            fade = tensor(c, "fade", [1, 2])
            prob1 = tensor(c, "prob1", [W, GROUP])
            prob2 = tensor(c, "prob2", [W, GROUP])
            prob_t = tensor(c, "prob_t", [P, TILES, W])
            prob_a = tensor(c, "prob_a", [P, TILES * W])
            row0 = tensor(c, "row0", [1, W])
            carry_in = tensor(c, "carry_in", [1, ZC])
            total = tensor(c, "total", [W, ZC])
            weight = tensor(c, "weight", [W, 1])
            inverse = tensor(c, "inverse", [W, 1])
            h_out = tensor(c, "h_out", [W, RING, D])
            ps_m = [bank(c, f"ps_m{i}", 1024, W) for i in range(2)]
            ps_p1 = bank(c, "ps_p1")
            ps_p2 = bank(c, "ps_p2")
            ps_o = bank(c, "ps_o")
            ps_cm = ps_o[:, 256:258]
            ps_ca = bank(c, "ps_ca")
            const1 = sem(c, "const1")
            index_set = sem(c, "index_set")
            sel_in = [sem(c, f"sel_in{half}") for half in range(2)]
            loads_in = [sem(c, f"loads_in{u}") for u in range(RING)]
            rows_in = [sem(c, f"rows_in{u}") for u in range(RING)]
            product_set, r_set, logit_set, scored, top_set, topq_set, topl_set, peak_set, bias1_set, bias2_set = (
                sem(c, n) for n in ("product_set", "r_set", "logit_set", "scored", "top_set", "topq_set", "topl_set",
                                    "peak_set", "bias1_set", "bias2_set"))
            peak_carried, valid_set, carried_set, fade_set, prob_set, prob_turned, prob_t_set = (
                sem(c, n) for n in ("peak_carried", "valid_set", "carried_set", "fade_set", "prob_set", "prob_turned",
                                    "prob_t_set"))
            total_carried, carry_set, summed, total_set, weight_set, inverse_set, h_set, h_free = (
                sem(c, n) for n in ("total_carried", "carry_set", "summed1", "total_set", "weight_set", "inverse_set",
                                    "h_set", "h_free"))
            prob_copied = sem(c, "prob_copied")
            h_stored = [sem(c, f"h_stored{u}") for u in range(2)]
            CONSTS = 5
            block = c.enter_context(nc.Block())
            ea_v = ea64.rearrange("(g p j) k -> g p (j k)", p=P, j=TILES)

            @block.sync
            def _(sp):
                n = iterations(sp)

                def load(entry, u):
                    g = group_of(sp, entry)
                    b = base_of(sp, entry)
                    for to, of in ((edge_f[:, u, :, :].rearrange("p j k -> p (j k)"), ea_v[bass.ds(g, 1)].rearrange("a p k -> (a p) k")),
                                   (pen_e[1:ROWS, u, :], pen_edge[:, bass.ds(g * GROUP, GROUP)]),
                                   (pen_n[:, u, :], pen_node[:, bass.ds(b, W)]),
                                   (q_win[:, u:u + 1], q_table[bass.ds(b, W), :])):
                        sp.dma_start(to, of).then_inc(loads_in[u], 16)

                def load_sel(s, half):
                    sp.dma_start(sel[:, half * HALF:(half + 1) * HALF], carry_sel[0:W, bass.ds(s, HALF)]).then_inc(sel_in[half], 16)

                first = steps_from(mybir.EngineType.SP, 0, RING)
                for u in range(RING):
                    if u % HALF == 0:
                        load_sel(u, u // HALF)
                    load(first[u], u)
                sp.wait_ge(h_set, 1)
                sp.dma_start(h_table[spare:spare + W, :], h_out[:, RING - 1, :]).then_inc(h_stored[1], 16)
                with sp.Fori(0, n) as i:
                    steps = steps_from(mybir.EngineType.SP, i * RING, 2 * RING)
                    for u in range(RING):
                        s = i * RING + u
                        sp.wait_ge(total_carried, s + 1)
                        alone(sp)
                        if u % HALF == HALF - 1:
                            load_sel(s + (RING + 1 - HALF), u // HALF)
                        load(steps[u + RING], u)
                        b = base_of(sp, steps[u])
                        sp.wait_ge(h_set, s + 2)
                        alone(sp)
                        sp.wait_ge(h_stored[(u + 1) % 2], i * (RING // 2 * 16) + 16 * (1 + u // 2))
                        sp.sem_inc(h_free, 1)
                        sp.dma_start(h_table[bass.ds(b, W), :], h_out[:, u, :]).then_inc(h_stored[u % 2], 16)
                for u in range(RING):
                    sp.wait_ge(loads_in[u], n * 64 + 64)
                for half in range(2):
                    sp.wait_ge(sel_in[half], n * 16 + 16)
                sp.wait_ge(h_stored[1], n * (RING // 2 * 16) + 16)
                sp.wait_ge(h_stored[0], n * (RING // 2 * 16))
                alone(sp)

            @block.gpsimd
            def _(pool):
                n = iterations(pool)

                def gather(s, u):
                    pool.wait_ge(index_set, s + 1)
                    alone(pool)
                    for j in range(TILES):
                        pool.indirect_dma_start(rows[:, u, j, 0:Z], None, z_table,
                                                bass.IndirectOffsetOnAxis(ap=index[:, u, j:j + 1], axis=0)).then_inc(rows_in[u], 16)

                pool.sem_inc(summed, HALF)
                for u in range(HALF):
                    gather(u, u)
                with pool.Fori(0, n) as i:
                    for u in range(RING):
                        pool.wait_ge(summed, i * RING + (u + 1))
                        alone(pool)
                        gather(i * RING + (u + HALF), (u + HALF) % RING)
                for u in range(HALF):
                    pool.wait_ge(rows_in[u], n * 80 + 80)
                    alone(pool)

            @block.scalar
            def _(act):
                n = iterations(act)

                def exps(s, u):
                    act.wait_ge(bias2_set, s + 1)
                    act.activation(fade[:, u % 2:u % 2 + 1], peak[0:1, 0:1], ACT.Exp, bias=carried[0:1, :], scale=-1.0).then_inc(fade_set, 1)
                    act.activation(prob1[:, :], ps_m[u % 2][:, 0:GROUP], ACT.Exp, bias=bias1[:, :])
                    act.activation(prob2[:, :], ps_m[u % 2][:, 0:GROUP], ACT.Exp, bias=bias2[:, :], scale=0.2).then_inc(prob_set, 1)

                def set_h(s, u):
                    act.wait_ge(inverse_set, s + 1)
                    act.wait_ge(h_free, s + 1)
                    act.activation(h_out[:, u % RING, :], total[:, 0:D], ACT.Copy, scale=inverse[:, 0:1]).then_inc(h_set, 1)

                act.wait_ge(const1, CONSTS)
                exps(0, 0)
                with act.Fori(0, n) as i:
                    for u in range(RING):
                        s = i * RING + u
                        set_h(s, u + RING - 1)
                        act.wait_ge(prob_turned, s * 2 + 1)
                        act.activation(prob_a[:, :], ps_p1[:, 0:TILES * W], ACT.Copy).then_inc(prob_copied, 1)
                        act.wait_ge(total_carried, s + 1)
                        act.wait_ge(fade_set, s + 1)
                        act.activation(carry_in[:, :], ps_ca[0:1, 0:ZC], ACT.Copy, scale=fade[0:1, u % 2:u % 2 + 1]).then_inc(carry_set, 1)
                        exps(s + 1, u + 1)
                set_h(n * RING, RING - 1)

            @block.tensor
            def _(pe):
                n = iterations(pe)

                def score(s, u, count):
                    pe.wait_ge(loads_in[u], count)
                    pe.wait_ge(logit_set, s + 1)
                    for lo, hi in ((0, 4), (4, 5)):
                        pe.matmul(ps_m[u % 2][:, lo * P:hi * P], pen_n[:, u, :], pen_e[:, u, lo * P:hi * P],
                                  start=True, stop=False)
                    for j in range(TILES):
                        ins = pe.matmul(ps_m[u % 2][:, j * P:(j + 1) * P], logit[:, u % 2, j:j + 1].to_broadcast([P, W]), ident[:, :],
                                        start=False, stop=(j >= 3))
                    ins.then_inc(scored, 1)

                def carry_peak(s, u, i):
                    pe.wait_ge(peak_set, s)
                    alone(pe)
                    pe.wait_ge(total_set, s)
                    alone(pe)
                    if u % HALF == 0:
                        pe.wait_ge(sel_in[u // HALF], i * 16 + 16 * (1 if u else 2))
                        alone(pe)
                    pe.matmul(ps_cm[0:1, :], sel[:, u:u + 1], peak[:, :], start=True, stop=True).then_inc(peak_carried, 1)

                pe.wait_ge(const1, CONSTS)
                pe.wait_ge(sel_in[0], 16)
                pe.matmul(ps_cm[0:1, :], sel[:, 0:1], peak[:, :], start=True, stop=True).then_inc(peak_carried, 1)
                score(0, 0, 64)
                score(1, 1, 64)
                with pe.Fori(0, n) as i:
                    for u in range(RING):
                        s = i * RING + u
                        pe.wait_ge(prob_set, s + 1)
                        alone(pe)
                        for prob, ps in ((prob1, ps_p1), (prob2, ps_p2)):
                            for j in range(TILES):
                                ins = pe.transpose(ps[:, j * W:(j + 1) * W], prob[:, j * P:(j + 1) * P], ident[0:W, 0:W])
                            ins.then_inc(prob_turned, 1)
                        carry_peak(s + 1, (u + 1) % RING, i)
                        pe.matmul(ps_ca[0:1, 0:ZC], sel[:, u:u + 1], total[:, :], start=True, stop=True).then_inc(total_carried, 1)
                        score(s + 2, (u + 2) % RING, i * 64 + 64 * (1 + (u + 2) // RING))
                        pe.wait_ge(carried_set, s + 2)
                        pe.wait_ge(carry_set, s + 1)
                        pe.wait_ge(prob_t_set, s + 1)
                        for j in range(TILES):
                            pe.matmul(ps_o[0:W, 0:ZC], prob_t[:, j, :], rows[:, u, j, :], start=(j == 0), stop=False)
                        pe.matmul(ps_o[0:W, 0:ZC], row0[:, :], carry_in[:, :], start=False, stop=True).then_inc(summed, 1)

            @block.vector
            def _(v):
                n = iterations(v)

                def set_index(entry, u):
                    g = group_of(v, entry)
                    v.tensor_copy(index[:, u, :], src_e[:, bass.ds(g * TILES, TILES)]).then_inc(index_set, 1)

                first = steps_from(mybir.EngineType.DVE, 0, RING)
                for u in range(RING):
                    set_index(first[u], u)

                v.sem_inc(total_set, 1)
                v.sem_inc(h_free, RING)
                v.memset(inverse[:, :], 1.0).then_inc(inverse_set, 1)
                v.memset(rows[:, :, :, Z:ZC], 1.0).then_inc(const1, 1)
                v.memset(pen_e[0:1, :, :], 1.0).then_inc(const1, 1)
                v.memset(peak[:, :], 1.0).then_inc(const1, 1)
                v.memset(carried[:, :], FLOOR)
                v.memset(total[:, :], 0.0).then_inc(const1, 1)
                v.tensor_copy(row0[:, :], ident[0:1, 0:W]).then_inc(const1, 1)
                v.wait_ge(const1, CONSTS)

                def edge_parts(s, u, loads):
                    v.wait_ge(loads_in[u], loads)
                    v.tensor_tensor(product[:, :, :], edge_f[:, u, :, :],
                                    v_edge[:, :].unsqueeze(1).to_broadcast([P, TILES, K64]), ALU.mult).then_inc(product_set, 1)
                    v.wait_ge(product_set, s + 1)
                    v.tensor_reduce(edge_r[:, :], product[:, :, :], AX.X, ALU.add).then_inc(r_set, 1)

                def logits(s, u, gathered):
                    v.wait_ge(r_set, s + 1)
                    v.wait_ge(rows_in[u], gathered)
                    v.tensor_tensor(logit[:, u % 2, :], edge_r[:, :], rows[:, u, :, D], ALU.add).then_inc(logit_set, 1)

                def raw_peaks(s, u):
                    v.wait_ge(scored, s + 1)
                    v.tensor_reduce(top[:, :], ps_m[u % 2][:, 0:GROUP], AX.X, ALU.max).then_inc(top_set, 1)

                def weights(s, u):
                    v.wait_ge(prob_turned, s * 2 + 2)
                    v.wait_ge(prob_copied, s + 1)
                    v.tensor_tensor(prob_t[:, :, :].rearrange("p j w -> p (j w)"), prob_a[:, :],
                                    ps_p2[:, 0:TILES * W], ALU.max).then_inc(prob_t_set, 1)

                def peaks(s, u):
                    q = q_win[:, u:u + 1]
                    v.wait_ge(peak_carried, s + 1)
                    v.tensor_scalar(valid[:, :], ps_cm[0:1, 1:2], 1.0, -FLOOR, ALU.subtract, ALU.mult).then_inc(valid_set, 1)
                    v.wait_ge(top_set, s + 1)
                    v.tensor_tensor(top_q[:, :], top[:, :], q, ALU.add).then_inc(topq_set, 1)
                    v.wait_ge(valid_set, s + 1)
                    v.tensor_tensor(carried[0:1, :], valid[:, :], ps_cm[0:1, 0:1], ALU.add).then_inc(carried_set, 1)
                    v.wait_ge(topq_set, s + 1)
                    v.scalar_tensor_tensor(out=top_l[:, :], in0=top_q[:, :], scalar=0.2, in1=top_q[:, :], op0=ALU.mult,
                                           op1=ALU.max).then_inc(topl_set, 1)
                    v.wait_ge(topl_set, s + 1)
                    v.wait_ge(carried_set, s + 1)
                    v.tensor_tensor(peak[:, 0:1], top_l[:, :], carried[:, :], ALU.max).then_inc(peak_set, 1)
                    v.wait_ge(peak_set, s + 1)
                    v.tensor_tensor(bias1[:, :], q, peak[:, 0:1], ALU.subtract).then_inc(bias1_set, 1)
                    v.scalar_tensor_tensor(out=bias2[:, :], in0=q, scalar=0.2, in1=peak[:, 0:1], op0=ALU.mult,
                                           op1=ALU.subtract).then_inc(bias2_set, 1)

                for u in range(2):
                    edge_parts(u, u, 64)
                    logits(u, u, 80)
                raw_peaks(0, 0)
                peaks(0, 0)
                raw_peaks(1, 1)
                edge_parts(2, 2, 64)
                logits(2, 2, 80)
                with v.Fori(0, n) as i:
                    for u in range(RING):
                        s = i * RING + u
                        u1, u2, u3 = ((u + k) % RING for k in (1, 2, 3))
                        turn = 1 + (u + 3) // RING
                        weights(s, u)
                        peaks(s + 1, u1)
                        edge_parts(s + 3, u3, i * 64 + 64 * turn)
                        v.wait_ge(summed, s + (HALF + 1))
                        v.tensor_copy(total[:, :], ps_o[0:W, 0:ZC]).then_inc(total_set, 1)
                        v.wait_ge(total_set, s + 2)
                        s_col = total[:, ZC - 1:ZC]
                        v.scalar_tensor_tensor(out=weight[:, :], in0=s_col, scalar=0.0, in1=s_col, op0=ALU.is_equal,
                                               op1=ALU.add).then_inc(weight_set, 1)
                        v.wait_ge(weight_set, s + 1)
                        v.reciprocal(inverse[:, :], weight[:, :]).then_inc(inverse_set, 1)
                        logits(s + 3, u3, i * 80 + 80 * turn)
                        if u == 0:
                            ahead = steps_from(mybir.EngineType.DVE, i * RING + RING, RING)
                        set_index(ahead[u], u)
                        raw_peaks(s + 2, u2)

        with ExitStack() as c:
            step = max(1, x_blocks // 10)
            parts = x_blocks // step
            h_in = tensor(c, "h_in", [x_part, x_blocks, D])
            h_loaded = [sem(c, f"h_loaded{t}") for t in range(parts)]
            out_set, out_stored = sem(c, "out_set"), sem(c, "out_stored")
            block = c.enter_context(nc.Block())

            @block.sync
            def _(sp):
                h_v = h_table[0:n_nodes].rearrange("(p b) d -> p b d", p=x_part)
                for t in range(parts):
                    sp.dma_start(h_in[:, t * step:(t + 1) * step, :], h_v[:, t * step:(t + 1) * step, :]).then_inc(h_loaded[t], 16)

            @block.vector
            def _(v):
                for t in range(parts):
                    v.wait_ge(h_loaded[t], 16)
                    h = h_in[:, t * step:(t + 1) * step, :]
                    v.tensor_tensor(h, h, xn[:, t * step:(t + 1) * step, :], ALU.add).then_inc(out_set, 1)

            @block.scalar
            def _(act):
                o_v = out.rearrange("(p b) d -> p b d", p=x_part)
                for t in range(parts):
                    act.wait_ge(out_set, t + 1)
                    act.dma_start(o_v[:, t * step:(t + 1) * step, :], h_in[:, t * step:(t + 1) * step, :]).then_inc(out_stored, 16)
                act.wait_ge(out_stored, 16 * parts)


def lay_out(x, src, dst, edge_attr_16, edge_attr_64, L0_gnn_W_emb, L0_gnn_b_emb, L0_gnn_W_lin, L0_gnn_b_lin,
            L1_gnn_Wn, L1_gnn_We, L1_gnn_Wa):
    groups = dst.shape[0] // GROUP
    return {
        "x": x,
        "src": src.reshape(groups, P, TILES).transpose(1, 0, 2),
        "dst": dst.reshape(groups, P, TILES).transpose(1, 0, 2),
        "dst_rows": dst.reshape(groups, P, TILES).transpose(0, 2, 1),
        "ea16": edge_attr_16.reshape(groups, P, TILES, -1).transpose(0, 2, 3, 1),
        "ea64": edge_attr_64,
        "w_emb": L0_gnn_W_emb, "b_emb": L0_gnn_b_emb, "w_lin": L0_gnn_W_lin, "b_lin": L0_gnn_b_lin,
        "wn": L1_gnn_Wn, "we": L1_gnn_We, "wa": L1_gnn_Wa,
    }


def kernel(**inputs):
    import numpy as np
    import concourse.bacc as bacc
    from concourse.bass_utils import run_bass_kernel_spmd

    nc = bacc.Bacc("TRN2", target_bir_lowering=False, num_devices=1)
    arrays, args = {}, []
    for name, a in lay_out(**inputs).items():
        a = np.ascontiguousarray(a)
        arrays[f"in_{name}"] = a
        args.append(nc.dram_tensor(f"in_{name}", a.shape, mybir.dt.from_np(a.dtype), kind="ExternalInput").ap())
    out = nc.dram_tensor("out_0", arrays["in_x"].shape, F32, kind="ExternalOutput").ap()
    bass_gnn(nc, *args, out)
    r = run_bass_kernel_spmd(nc, [arrays], core_ids=[0])
    return r.results[0]["out_0"]
```
